# Optimizing a Trainium2 kernel written in Bass

```python
import numpy as np
import jax
import jax.numpy as jnp

def _softmax(x, axis=-1):
    return jax.nn.softmax(x, axis=axis)

def _gelu(x):
    return jax.nn.gelu(x, approximate=True)

def _silu(x):
    return jax.nn.silu(x)

def _sigmoid(x):
    return jax.nn.sigmoid(x)

def _layernorm(x, axis=-1, eps=1e-05):
    m = jnp.mean(x, axis=axis, keepdims=True)
    v = jnp.var(x, axis=axis, keepdims=True)
    return (x - m) / jnp.sqrt(v + eps)

def _scatter_add(tgt, idx, src, axis=0):
    return tgt.at[idx].add(src)

def _segment_sum(src, seg, n):
    return jax.ops.segment_sum(src, seg, n)
kernel_name = 'mk_xattn_seq_d1_seqx_r2_822750'

def setup_inputs(seed: int=0):
    np.random.seed(seed)
    _w = jnp.asarray

    def _rec_inputs():
        import jax
        import jax.numpy as jnp
        _rk = jax.random.key(seed)
        x = -0.0002928 + 1 * jax.random.normal(jax.random.fold_in(_rk, 1), (16, 512, 512), jnp.float32)
        _lenS = 512 - jax.random.randint(jax.random.fold_in(_rk, 7), (16,), 0, max(1, 512 // 4) + 1, jnp.int32)
        _lenS2 = 512 - jax.random.randint(jax.random.fold_in(_rk, 8), (16,), 0, max(1, 512 // 4) + 1, jnp.int32)
        _ctx_1024P = jax.random.normal(jax.random.fold_in(_rk, 11), (16, 16, 512), jnp.float32)
        _ctx_1024c = jax.random.dirichlet(jax.random.fold_in(_rk, 511), 0.3 * jnp.ones((16,), jnp.float32), (16, 512))
        _ctx_1024t = jnp.einsum('bsk,bkd->bsd', _ctx_1024c, _ctx_1024P)
        _ctx_1024t = _ctx_1024t * jax.lax.rsqrt(jnp.mean(jnp.square(_ctx_1024t)) + 1e-12) * 0.953939
        ctx_1024 = -1.39393e-06 + 0.999914 * (_ctx_1024t + 0.3 * jax.random.normal(jax.random.fold_in(_rk, 611), (16, 512, 512), jnp.float32))
        _validS = jnp.arange(512)[None, :] < _lenS[:, None]
        _validS2 = jnp.arange(512)[None, :] < _lenS2[:, None]
        _causal = jnp.tril(jnp.ones((512, 512), dtype=bool))
        mask_Bx1xSxS2_fk1 = jnp.where(jnp.broadcast_to(_validS2[:, None, None, :], (16, 1, 512, 512)), 1.0, 0.0).astype(jnp.float32)
        return (x, ctx_1024, mask_Bx1xSxS2_fk1)
    x, ctx_1024, mask_Bx1xSxS2_fk1 = _rec_inputs()

    def _L0_xattn_setup():
        import jax, jax.numpy as jnp
        import numpy as np
        B, S, D = (2, 1024, 512)
        H, DH = (16, 64)
        LN_EPS = 1e-05
        key = jax.random.key(seed)
        ks = jax.random.split(key, 12)
        scale = 1.0 / np.sqrt(D)
        inp = {'q': jax.random.normal(ks[0], (B, S, D), jnp.float32), 'k': jax.random.normal(ks[1], (B, S, D), jnp.float32), 'v': jax.random.normal(ks[2], (B, S, D), jnp.float32), 'mask': (jax.random.uniform(ks[3], (B, 1, S, S)) < 0.9).astype(jnp.float32), 'Wq': jax.random.normal(ks[4], (D, H * DH), jnp.float32) * scale, 'bq': jnp.zeros((H * DH,), jnp.float32), 'Wk': jax.random.normal(ks[5], (D, H * DH), jnp.float32) * scale, 'bk': jnp.zeros((H * DH,), jnp.float32), 'Wv': jax.random.normal(ks[6], (D, H * DH), jnp.float32) * scale, 'bv': jnp.zeros((H * DH,), jnp.float32), 'Wo': jax.random.normal(ks[7], (H * DH, D), jnp.float32) * scale, 'bo': jnp.zeros((D,), jnp.float32), 'gamma': jnp.ones((D,), jnp.float32), 'beta': jnp.zeros((D,), jnp.float32)}
        return inp
    _L0_xattn_all = _L0_xattn_setup()
    _L0_xattn_in = {k: v for k, v in _L0_xattn_all.items() if k in ('Wq', 'bq', 'Wk', 'bk', 'Wv', 'bv', 'Wo', 'bo', 'gamma', 'beta')}
    del _L0_xattn_all
    return {'x': x, 'ctx_1024': ctx_1024, 'mask_Bx1xSxS2_fk1': mask_Bx1xSxS2_fk1, 'L0_xattn_Wq': _L0_xattn_in['Wq'], 'L0_xattn_bq': _L0_xattn_in['bq'], 'L0_xattn_Wk': _L0_xattn_in['Wk'], 'L0_xattn_bk': _L0_xattn_in['bk'], 'L0_xattn_Wv': _L0_xattn_in['Wv'], 'L0_xattn_bv': _L0_xattn_in['bv'], 'L0_xattn_Wo': _L0_xattn_in['Wo'], 'L0_xattn_bo': _L0_xattn_in['bo'], 'L0_xattn_gamma': _L0_xattn_in['gamma'], 'L0_xattn_beta': _L0_xattn_in['beta']}

def reference(x, ctx_1024, mask_Bx1xSxS2_fk1, L0_xattn_Wq, L0_xattn_bq, L0_xattn_Wk, L0_xattn_bk, L0_xattn_Wv, L0_xattn_bv, L0_xattn_Wo, L0_xattn_bo, L0_xattn_gamma, L0_xattn_beta):
    import jax
    import jax.numpy as jnp

    def _L0_xattn_ref(q, k, v, mask, Wq, bq, Wk, bk, Wv, bv, Wo, bo, gamma, beta):
        import jax, jax.numpy as jnp
        import numpy as np
        B, S, D = (2, 1024, 512)
        H, DH = (16, 64)
        LN_EPS = 1e-05
        b, s, _ = q.shape
        Q = (q @ Wq + bq).reshape(b, s, H, DH).transpose(0, 2, 1, 3)
        K = (k @ Wk + bk).reshape(b, s, H, DH).transpose(0, 2, 1, 3)
        V = (v @ Wv + bv).reshape(b, s, H, DH).transpose(0, 2, 1, 3)
        scores = jnp.einsum('bhqd,bhkd->bhqk', Q, K) / jnp.sqrt(jnp.float32(DH))
        scores = scores * mask
        attn = jax.nn.softmax(scores, axis=-1)
        ctx = jnp.einsum('bhqk,bhkd->bhqd', attn, V)
        ctx = ctx.transpose(0, 2, 1, 3).reshape(b, s, H * DH)
        out = ctx @ Wo + bo
        x = q + out
        mu = jnp.mean(x, axis=-1, keepdims=True)
        var = jnp.var(x, axis=-1, keepdims=True)
        return (x - mu) * jax.lax.rsqrt(var + LN_EPS) * gamma + beta
    x = _L0_xattn_ref(x, ctx_1024, ctx_1024, mask_Bx1xSxS2_fk1, L0_xattn_Wq, L0_xattn_bq, L0_xattn_Wk, L0_xattn_bk, L0_xattn_Wv, L0_xattn_bv, L0_xattn_Wo, L0_xattn_bo, L0_xattn_gamma, L0_xattn_beta)
    return x

_drawn_inputs = setup_inputs


def setup_inputs(seed=0):
    import zlib

    import numpy as np

    out = dict(_drawn_inputs(seed))
    spreads = {'L0_xattn_bq': (0.0, 0.35),
     'L0_xattn_bk': (0.0, 2.0),
     'L0_xattn_bv': (0.0, 0.1),
     'L0_xattn_bo': (0.0, 0.1),
     'L0_xattn_gamma': (1.0, 0.2),
     'L0_xattn_beta': (0.0, 0.1)}
    factors = {}
    for name, (base, spread) in spreads.items():
        noise = np.random.default_rng([zlib.crc32(name.encode()), seed]).standard_normal(out[name].shape)
        drawn = base * np.exp(spread * noise) if base else spread * noise
        out[name] = jnp.asarray(drawn.astype(out[name].dtype))
    for name, factor in factors.items():
        out[name] = (out[name] * factor).astype(out[name].dtype)
    return out
```

```python
from contextlib import ExitStack

import concourse.bass as bass
from concourse import mybir

F32 = mybir.dt.float32
F32R = mybir.dt.float32r
ALU = mybir.AluOpType
ACT = mybir.ActivationFunctionType

P = 128
B, S, D = 16, 512, 512
H, DH = 16, 64
GROUPS = 2
GH = H // GROUPS
GW = GH * DH
PAIRS = GH // 2
QT, KT, DT = S // P, S // P, D // P
SCORE_SCALE = 1.0 / 8.0
LN_EPS = 1e-05
RAW_SLOTS = 4
NX = QT + KT
NSTAGED = NX + KT
DMA = 16

SCORE_BANKS, PT_BANKS, FREE_STAGES = 2, 2, 2
CTX_BANKS = 1

FILL_SCHEDULE = [
    (0, 1, "K", 2), (0, 3, "B", 0), (0, 4, "B", 1), (0, 5, "B", 2), (0, 6, "B", 3),
    (1, 1, "Q", 2),
    (2, 0, "K", 3), (2, 2, "Q", 3),
    (3, 0, "X", 0), (3, 1, "X", 1), (3, 2, "X", 2), (3, 3, "X", 3),
    (3, 4, "X", 4), (3, 5, "X", 5), (3, 6, "X", 6), (3, 7, "X", 7),
    (4, 1, "K", 0), (4, 4, "A", 0), (4, 6, "A", 1),
    (5, 0, "Q", 0), (5, 2, "A", 2), (5, 4, "A", 3),
    (6, 0, "K", 1), (6, 2, "Q", 1),
    (7, 4, "V", 0), (7, 5, "V", 1), (7, 6, "V", 2), (7, 7, "V", 3),
]
FILL_BANKS = 3
FILL_BANK = {(kind, k): n % FILL_BANKS for n, (_, _, kind, k) in enumerate(FILL_SCHEDULE)}


def is_ahead(kind, k):
    return kind in "XV" or (kind in "KQ" and k < 2)


def fills(slot, step, first, last):
    for s, t, kind, k in FILL_SCHEDULE:
        if (s, t) != (slot, step):
            continue
        if (kind == "B" and first) or (is_ahead(kind, k) and last):
            continue
        yield kind, k


def cross_attention(nc, x, c, mask, wq, bq, wk, bk, wv, bv, wo, bo, gamma, beta, out):
    ctx = ExitStack()
    with ctx:
        def sb(name, shape, dt=F32):
            return ctx.enter_context(nc.sbuf_tensor(name, shape, dt))

        def ps(name, shape):
            return ctx.enter_context(nc.psum_tensor(name, shape, F32))

        def sem(name):
            return ctx.enter_context(nc.semaphore(name))

        partial = nc.dram_tensor("partial", (B, S, D), F32, kind="Internal").ap()

        w_hi = {w: sb(f"w{w}_hi", [P, DT, GW], F32R) for w in "qkv"}
        w_lo = {w: sb(f"w{w}_lo", [P, DT, GW], F32R) for w in "qkv"}
        w_hi["o"] = sb("wo_hi", [P, PAIRS, D], F32R)
        w_lo["o"] = sb("wo_lo", [P, PAIRS, D], F32R)
        xT = {t: (sb(f"{t}T_hi", [P, DT, S], F32R), sb(f"{t}T_lo", [P, DT, S], F32R)) for t in "cx"}
        q_stack = sb("q_stack", [P, 2, 2, S], F32R)
        k_twice = sb("k_twice", [P, 2, 2, 2, S], F32R)
        v_sb = sb("v_sb", [P, KT, 2 * GW], F32R)
        mask_sb = sb("mask_sb", [P, QT, S])
        acc = sb("acc", [P, QT, D])
        raw = sb("raw", [P, RAW_SLOTS, D])
        stage = sb("stage", [P, 2, S])
        probs = sb("probs", [P, 2, QT, S])
        pT_hi = sb("pT_hi", [P, KT, S], F32R)
        pT_lo = sb("pT_lo", [P, KT, S], F32R)
        ctxT_hi = sb("ctxT_hi", [P, 2, S], F32R)
        ctxT_lo = sb("ctxT_lo", [P, 2, S], F32R)
        ctxT = sb("ctxT", [P, S])
        gamma_b, beta_b, bo_b = sb("gamma_b", [P, D]), sb("beta_b", [P, D]), sb("bo_b", [P, D])
        ident = sb("ident", [P, P])
        bias_col = {n: sb(f"b{n}_col", [P, GROUPS * PAIRS]) for n in "qkv"}
        row_max, neg_max = sb("row_max", [P, 2, QT]), sb("neg_max", [P, 2, QT])
        row_sum, inv_sum = sb("row_sum", [P, 2, QT]), sb("inv_sum", [P, 2, QT])
        stats, moments = sb("stats", [P, QT, 6]), sb("moments", [P, QT, 2])
        eps4, half4 = sb("eps4", [P, QT]), sb("half4", [P, QT])
        var_eps, rstd = sb("var_eps", [P, QT]), sb("rstd", [P, QT])

        score_ps = ps("score_ps", [P, SCORE_BANKS, S])
        pT_ps = ps("pT_ps", [P, PT_BANKS, S])
        ctx_ps = ps("ctx_ps", [P, S])
        fill_ps = ps("fill_ps", [P, FILL_BANKS, S])

        consts_in = sem("consts_in")
        consts_set = sem("consts_set")
        w_in = {w: sem(f"w_in_{w}") for w in "qkvo"}
        w_hi_done = sem("w_hi_done")
        w_split = sem("w_split")
        raw_in = [sem(f"raw_in{r}") for r in range(RAW_SLOTS)]
        mask_in = [sem(f"mask_in{q}") for q in range(QT)]
        acc_in = [sem(f"acc_in{q}") for q in range(QT)]
        stored = [sem(f"stored{q}") for q in range(QT)]
        x_ready = sem("x_ready")
        v_ready = sem("v_ready")
        staged = sem("staged")
        stage_hi = sem("stage_hi")
        stage_split = sem("stage_split")
        qk_ready = sem("qk_ready")
        qk_hi = sem("qk_hi")
        qk_lo = sem("qk_lo")
        k_dup = [[sem(f"k_dup{i}{a}") for a in "ab"] for i in range(2)]
        s_ready = sem("s_ready")
        masked = sem("masked")
        max_negated = sem("max_negated")
        exp_done = sem("exp_done")
        sum_inverted = sem("sum_inverted")
        p_ready = sem("p_ready")
        t_ready = sem("t_ready")
        pT_hi_done = sem("pT_hi_done")
        pT_split = sem("pT_split")
        pv_ready = sem("pv_ready")
        ctx_crossed = sem("ctx_crossed")
        ctx_added = sem("ctx_added")
        ctx_hi_done = sem("ctx_hi_done")
        ctx_split = sem("ctx_split")
        out_ready = sem("out_ready")
        acc_added = sem("acc_added")
        bo_added = sem("bo_added")
        stats_done = sem("stats_done")
        moments_done = sem("moments_done")
        eps_added = sem("eps_added")
        rstd_done = sem("rstd_done")
        centered = sem("centered")
        normed = sem("normed")
        waits_passed = sem("waits_passed")

        def staged_no(n, kind, k):
            return n * NSTAGED + (k if kind == "X" else NX + k) + 1

        def qk_no(n, kind, p):
            return n * 2 * PAIRS + 2 * p + (kind == "Q") + 1

        def out_no(n, kind, q):
            return n * 2 * QT + (q if kind == "A" else QT + q) + 1

        def fill_read(n, kind, k):
            if kind in "XV":
                return staged, staged_no(n, kind, k)
            if kind in "KQ":
                return qk_lo, qk_no(n, kind, k)
            return acc_added, out_no(n, kind, k)

        def batch_of(it, kind, k):
            if kind == "B":
                return it - 1
            return it + 1 if is_ahead(kind, k) else it

        def batches(eng, prologue, body, epilogue):
            for g in range(GROUPS):
                prologue(g)
                body(g, 0, True, False)
                with eng.Fori(1, B - 1) as b:
                    body(g, b, False, False)
                body(g, B - 1, False, True)
                epilogue(g)

        def wait_alone(eng, semaphore, value):
            eng.wait_ge(semaphore, value)
            if not isinstance(value, int):
                eng.sem_inc(waits_passed, 1)

        def head_at(it, h, last):
            if h < GH:
                return it, h
            return (None, None) if last else (it + 1, h - GH)

        def v_part(tile, lo):
            view = v_sb[:, tile, :].rearrange("p (j a e) -> p j a e", a=4, e=DH)
            return view[:, :, 1:3, :] if lo else view[:, :, 0:4:3, :]

        block = ctx.enter_context(nc.Block())

        @block.sync
        def _(sp):
            for n, vec in (("q", bq), ("k", bk), ("v", bv)):
                with nc.allow_non_contiguous_dma(reason="once, 1024 values to columns"):
                    sp.dma_start(bias_col[n][:, :], vec.rearrange("(j p) -> p j", p=P)).then_inc(consts_in, DMA)
            for dst, vec in ((gamma_b, gamma), (beta_b, beta), (bo_b, bo)):
                sp.dma_start(dst[:, :], vec.partition_broadcast(P)).then_inc(consts_in, DMA)

            def load_raw(n, b, j):
                if isinstance(n, int) and n * NX + j < RAW_SLOTS:
                    pass
                else:
                    sp.wait_ge(x_ready, n * NX + j - RAW_SLOTS + 1)
                src, t = (c, j) if j < KT else (x, j - KT)
                sp.dma_start(raw[:, j % RAW_SLOTS, :], src[b, t * P:(t + 1) * P, :]).then_inc(
                    raw_in[j % RAW_SLOTS], DMA)

            def load_mask(n, b, q):
                if not (isinstance(n, int) and n == 0):
                    sp.wait_ge(masked, (n * GH - 1) * QT + q + 1 + SCORE_BANKS)
                sp.dma_start(mask_sb[:, q, :], mask[b, 0, q * P:(q + 1) * P, :]).then_inc(mask_in[q], DMA)

            def load_acc(g, it, b, q):
                if not (isinstance(it, int) and it == 0):
                    sp.wait_ge(stored[q], it * DMA)
                src = (x, partial)[g]
                sp.dma_start(acc[:, q, :], src[b, q * P:(q + 1) * P, :]).then_inc(acc_in[q], DMA)

            def store(g, it, b, q):
                if g == 0:
                    sp.wait_ge(acc_added, out_no(it, "B", q))
                else:
                    sp.wait_ge(normed, (it - B) * QT + q + 1)
                dst = (partial, out)[g]
                sp.dma_start(dst[b, q * P:(q + 1) * P, :], acc[:, q, :]).then_inc(stored[q], DMA)

            def prologue(g):
                if g:
                    sp.wait_ge(out_ready, out_no(g * B - 1, "B", QT - 1))
                cols = slice(g * GW, (g + 1) * GW)
                for i, (w, mat) in enumerate((("q", wq), ("k", wk), ("v", wv), ("o", wo))):
                    if i >= 2:
                        sp.wait_ge(w_split, 4 * g + i - 1)
                    src = mat[cols, :].rearrange("(j p) n -> p j n", p=P) if w == "o" else \
                        mat[:, cols].rearrange("(j p) n -> p j n", p=P)
                    sp.dma_start(probs[:, i % 2, :, :], src).then_inc(w_in[w], DMA)
                    if i < 2:
                        for j in range(4 * i, 4 * i + 4):
                            if i == 0:
                                load_raw(g * B, 0, j)
                for j in range(RAW_SLOTS, NX):
                    load_raw(g * B, 0, j)
                for q in range(QT):
                    load_mask(g * B, 0, q)

            def body(g, b, first, last):
                it = b + g * B
                if not last:
                    for j in range(RAW_SLOTS):
                        load_raw(it + 1, b + 1, j)
                for q in range(QT):
                    if not first:
                        store(g, it - 1, b - 1, q)
                if g == 0:
                    for q in range(QT):
                        load_acc(g, it, b, q)
                if not last:
                    for j in range(RAW_SLOTS, NX):
                        load_raw(it + 1, b + 1, j)
                if g == 1:
                    for q in range(QT):
                        load_acc(g, it, b, q)
                if not last:
                    for q in range(QT):
                        load_mask(it + 1, b + 1, q)

            def epilogue(g):
                for q in range(QT):
                    store(g, g * B + B - 1, B - 1, q)

            batches(sp, prologue, body, epilogue)
            for q in range(QT):
                sp.wait_ge(stored[q], GROUPS * B * DMA)

        @block.tensor
        def _(pe):
            def three_products(bank, lhs, rhs, tiles, more=None):
                todo = [(a, r, t) for t in tiles for a, r in ((0, 0), (1, 0), (0, 1))]
                for n, (a, r, t) in enumerate(todo):
                    mm = nc.tensor.matmul(bank, lhs(a, t), rhs(r, t), start=(n == 0), stop=(n == len(todo) - 1))
                return mm

            def fill(n, kind, k, free):
                if free is not None:
                    pe.wait_ge(*free)
                bank = fill_ps[:, FILL_BANK[kind, k], :]
                if kind == "X":
                    pe.wait_ge(raw_in[k % RAW_SLOTS], (n * (NX // RAW_SLOTS) + k // RAW_SLOTS + 1) * DMA)
                    for t in range(DT):
                        mm = nc.tensor.transpose(bank[:, t * P:(t + 1) * P], raw[:, k % RAW_SLOTS, t * P:(t + 1) * P],
                                                 ident[:, :])
                    mm.then_inc(x_ready, 1)
                elif kind in "KQ":
                    if k == 0:
                        pe.wait_ge(stage_split, staged_no(n, "X", NX - 1 if kind == "Q" else KT - 1) + FREE_STAGES)
                    w = kind.lower()
                    act = xT["x" if kind == "Q" else "c"]
                    three_products(bank, lambda a, t: (w_hi, w_lo)[a][w][:, t, k * P:(k + 1) * P],
                                   lambda r, t: act[r][:, t, :], range(DT)).then_inc(qk_ready, 1)
                elif kind == "V":
                    three_products(bank, lambda a, t: xT["c"][a][:, t, k * P:(k + 1) * P],
                                   lambda r, t: (w_hi, w_lo)[r]["v"][:, t, :], range(DT)).then_inc(v_ready, 1)
                else:
                    pair0 = 0 if kind == "A" else 2
                    if k == 0:
                        pe.wait_ge(ctx_split, n * PAIRS + pair0 + 2)
                    three_products(bank, lambda a, t: (ctxT_hi, ctxT_lo)[a][:, t % 2, k * P:(k + 1) * P],
                                   lambda r, t: (w_hi, w_lo)[r]["o"][:, t, :], (pair0, pair0 + 1)).then_inc(out_ready, 1)

            def scores(n, h, q):
                par, ab = (h // 2) % 2, h % 2
                if q == 0:
                    pe.wait_ge(qk_lo, qk_no(n, "Q", h // 2))
                    pe.wait_ge(k_dup[par][ab], (n * 2 + h // 4 + 1) * DMA)
                pe.wait_ge(masked, (n * GH + h) * QT + q + 1)
                bank = score_ps[:, q % SCORE_BANKS, :]
                qs = q_stack[:, par, ab, q * P:(q + 1) * P]
                nc.tensor.matmul(bank, qs, k_twice[:, par, ab, 0, :], start=True, stop=False)
                nc.tensor.matmul(bank, qs, k_twice[:, par, ab, 1, :], start=False, stop=True).then_inc(s_ready, 1)

            def transposes(it, h, t):
                if t == 0:
                    pe.wait_ge(p_ready, (it * GH + h + 1) * QT)
                pe.wait_ge(pT_split, (it * GH + h) * KT + t + 1)
                for q in range(QT):
                    mm = nc.tensor.transpose(pT_ps[:, t % PT_BANKS, q * P:(q + 1) * P],
                                             probs[:, h % 2, q, t * P:(t + 1) * P], ident[:, :])
                mm.then_inc(t_ready, 1)

            def values(it, h, t):
                if h == 0 and t == 0:
                    pe.wait_ge(stage_split, staged_no(it, "V", KT - 1) + FREE_STAGES)
                if t == 0:
                    pe.wait_ge(ctx_added, it * GH + h + 1)
                pe.wait_ge(pT_split, (it * GH + h) * KT + t + 1 + PT_BANKS)
                v = v_sb[:, t, h * P:(h + 1) * P]
                nc.tensor.matmul(ctx_ps[:, :], v, pT_hi[:, t, :], start=(t == 0), stop=False)
                mm = nc.tensor.matmul(ctx_ps[:, :], v, pT_lo[:, t, :], start=False, stop=(t == KT - 1))
                if t == KT - 1:
                    mm.then_inc(pv_ready, 1)

            users = {}

            def prologue(g):
                n = g * B
                if g == 0:
                    pe.wait_ge(consts_set, 4)
                users.clear()
                for kind, k in [("X", j) for j in range(NX)] + [("K", 0), ("Q", 0), ("K", 1), ("Q", 1)] + \
                        [("V", t) for t in range(KT)]:
                    bank = FILL_BANK[kind, k]
                    free = users.get(bank)
                    if free is None and g:
                        free = (acc_added, out_no(n - 1, "B", QT - 1))
                    if (kind, k) == ("K", 0):
                        pe.wait_ge(w_split, 4 * g + 4)
                    fill(n, kind, k, free)
                    users[bank] = fill_read(n, kind, k)
                for h in range(2):
                    for q in range(QT):
                        scores(n, h, q)

            def body(g, b, first, last):
                it = b + g * B
                users.clear()
                users.update((FILL_BANK["V", t], fill_read(it, "V", t)) for t in range(KT))
                for slot in range(GH):
                    for step in range(8):
                        if step < 4:
                            transposes(it, slot, step)
                        else:
                            values(it, slot, step - 4)
                            n, h = head_at(it, slot + 2, last)
                            if n is not None:
                                scores(n, h, step - 4)
                        for kind, k in fills(slot, step, first, last):
                            n = batch_of(it, kind, k)
                            bank = FILL_BANK[kind, k]
                            fill(n, kind, k, users[bank])
                            users[bank] = fill_read(n, kind, k)

            def epilogue(g):
                it = g * B + B - 1
                for q in range(QT):
                    bank = FILL_BANK["B", q]
                    fill(it, "B", q, users[bank])
                    users[bank] = fill_read(it, "B", q)

            batches(pe, prologue, body, epilogue)

        @block.scalar
        def _(act):
            def evacuate(n, kind, k):
                bank = fill_ps[:, FILL_BANK[kind, k], :]
                if kind in "XV":
                    i = staged_no(n, kind, k)
                    act.wait_ge(*((x_ready, n * NX + k + 1) if kind == "X" else (v_ready, n * KT + k + 1)))
                    act.wait_ge(stage_split, i)
                    slot = (k if kind == "X" else NX + k) % 2
                    nc.scalar.activation(stage[:, slot, :], bank, ACT.Copy).then_inc(staged, 1)
                elif kind in "KQ":
                    act.wait_ge(qk_ready, qk_no(n, kind, k))
                    for ab, part in ((0, slice(0, DH)), (1, slice(DH, P))):
                        dst = k_twice[part, k % 2, ab, 0, :] if kind == "K" else q_stack[part, k % 2, ab, :]
                        last = nc.scalar.activation(dst, bank[part, :], ACT.Identity,
                                                    bias=bias_of(kind, n, k)[part, :])
                    last.then_inc(qk_hi, 1)

            group = [0]

            def bias_of(kind, n, k):
                col = group[0] * PAIRS + k
                return bias_col[kind.lower()][:, col:col + 1]

            def duplicate_keys(n, p):
                act.wait_ge(qk_lo, qk_no(n, "K", p))
                for ab, (a, z) in ((0, (slice(0, DH), slice(DH, P))), (1, (slice(DH, P), slice(0, DH)))):
                    act.dma_start(k_twice[z, p % 2, ab, :, :].bitcast(F32),
                                  k_twice[a, p % 2, ab, :, :].bitcast(F32)).then_inc(k_dup[p % 2][ab], DMA)

            def exponentials(n, h, half):
                act.wait_ge(max_negated, (n * GH + h) * 2 + half + 1)
                for q in (2 * half, 2 * half + 1):
                    nc.scalar.activation(probs[:, h % 2, q, :], probs[:, h % 2, q, :], ACT.Exp,
                                         bias=neg_max[:, h % 2, q:q + 1],
                                         accum_out=row_sum[:, h % 2, q:q + 1]).then_inc(exp_done, 1)

            def transposed_hi(it, h, t):
                act.wait_ge(t_ready, (it * GH + h) * KT + t + 1)
                nc.scalar.activation(pT_hi[:, t, :], pT_ps[:, t % PT_BANKS, :], ACT.Copy).then_inc(pT_hi_done, 1)

            def cross(it, h):
                act.wait_ge(pv_ready, it * GH + h + 1)
                if h % 2 == 0 and not (isinstance(it, int) and it == 0 and h == 0):
                    act.wait_ge(ctx_split, it * PAIRS + h // 2)
                dst, src = (slice(0, DH), slice(DH, P)) if h % 2 == 0 else (slice(DH, P), slice(0, DH))
                nc.scalar.activation(ctxT[dst, :], ctx_ps[src, :], ACT.Copy).then_inc(ctx_crossed, 1)

            def prologue(g):
                group[0] = g
                if g == 0:
                    act.wait_ge(consts_in, 6 * DMA)
                n = g * B
                for i, w in enumerate("qkvo"):
                    act.wait_ge(w_in[w], (g + 1) * DMA)
                    nc.scalar.activation(w_hi[w][:, :, :], probs[:, i % 2, :, :], ACT.Copy).then_inc(w_hi_done, 1)
                for j in range(NX):
                    evacuate(n, "X", j)
                for p in range(2):
                    evacuate(n, "K", p)
                    duplicate_keys(n, p)
                    evacuate(n, "Q", p)
                for t in range(KT):
                    evacuate(n, "V", t)
                exponentials(n, 0, 0)
                exponentials(n, 0, 1)
                exponentials(n, 1, 0)

            def body(g, b, first, last):
                it = b + g * B
                for slot in range(GH):
                    for step in range(8):
                        if step < 4:
                            transposed_hi(it, slot, step)
                        if step == 0 and slot > 0:
                            cross(it, slot - 1)
                        for at, ahead, half in ((1, 1, 1), (7, 2, 0)):
                            n, h = head_at(it, slot + ahead, last)
                            if step == at and n is not None:
                                exponentials(n, h, half)
                        for kind, k in fills(slot, step, first, last):
                            evacuate(batch_of(it, kind, k), kind, k)
                            if kind == "K":
                                duplicate_keys(batch_of(it, kind, k), k)
                cross(it, GH - 1)

            batches(act, prologue, body, lambda g: None)

        @block.vector
        def _(dve):
            nc.vector.sem_inc(masked, SCORE_BANKS)
            nc.vector.sem_inc(pT_split, PT_BANKS)
            nc.vector.sem_inc(ctx_added, CTX_BANKS)
            group = [0]

            def mask_and_max(n, h, q):
                if h == 0:
                    dve.wait_ge(mask_in[q], (n + 1) * DMA)
                wait_alone(dve, s_ready, (n * GH + h) * QT + q + 1)
                nc.vector.tensor_tensor_reduce(
                    out=probs[:, h % 2, q, :], in0=score_ps[:, q % SCORE_BANKS, :], in1=mask_sb[:, q, :],
                    scale=SCORE_SCALE, scalar=-3.0e38, op0=ALU.mult, op1=ALU.max,
                    accum_out=row_max[:, h % 2, q:q + 1]).then_inc(masked, 1)

            def invert_sums(n, h, half):
                dve.wait_ge(exp_done, (n * GH + h) * QT + 2 * half + 2)
                cols = slice(2 * half, 2 * half + 2)
                nc.vector.reciprocal(inv_sum[:, h % 2, cols], row_sum[:, h % 2, cols]).then_inc(sum_inverted, 1)

            def transposed_lo(it, h, t):
                dve.wait_ge(pT_hi_done, (it * GH + h) * KT + t + 1)
                nc.vector.tensor_tensor(pT_lo[:, t, :], pT_ps[:, t % PT_BANKS, :], pT_hi[:, t, :],
                                        ALU.subtract).then_inc(pT_split, 1)

            def add_context(it, h):
                dve.wait_ge(ctx_crossed, it * GH + h + 1)
                part = slice(0, DH) if h % 2 == 0 else slice(DH, P)
                col = group[0] * PAIRS + h // 2
                nc.vector.scalar_tensor_tensor(
                    out=ctxT[part, :], in0=ctx_ps[part, :], scalar=bias_col["v"][part, col:col + 1],
                    in1=ctxT[part, :], op0=ALU.add, op1=ALU.add).then_inc(ctx_added, 1)

            def evacuate(n, kind, k):
                bank = fill_ps[:, FILL_BANK[kind, k], :]
                if kind in "KQ":
                    dve.wait_ge(qk_hi, qk_no(n, kind, k))
                    col = group[0] * PAIRS + k
                    for ab, part, other in ((0, slice(0, DH), slice(DH, P)), (1, slice(DH, P), slice(0, DH))):
                        hi = k_twice[part, k % 2, ab, 0, :] if kind == "K" else q_stack[part, k % 2, ab, :]
                        lo = k_twice[part, k % 2, ab, 1, :] if kind == "K" else q_stack[other, k % 2, ab, :]
                        last = nc.vector.scalar_tensor_tensor(
                            out=lo, in0=bank[part, :], scalar=bias_col[kind.lower()][part, col:col + 1], in1=hi,
                            op0=ALU.add, op1=ALU.subtract)
                    last.then_inc(qk_lo, 1)
                elif kind in "AB":
                    dve.wait_ge(out_ready, out_no(n, kind, k))
                    if kind == "A":
                        dve.wait_ge(acc_in[k], (n + 1) * DMA)
                        if group[0] == 0:
                            dve.wait_ge(bo_added, n * QT + k + 1)
                    else:
                        dve.wait_ge(acc_added, out_no(n, "A", k))
                    nc.vector.tensor_tensor(acc[:, k, :], bank, acc[:, k, :], ALU.add).then_inc(acc_added, 1)

            def layer_norm(it, slot, step):
                n = it - B
                if slot == 1 and step < 4:
                    dve.wait_ge(acc_added, out_no(it, "B", step))
                    nc.vector.bn_stats(stats[:, step, :], acc[:, step, :]).then_inc(stats_done, 1)
                elif slot == 1:
                    q = step - 4
                    wait_alone(dve, stats_done, n * QT + q + 1)
                    nc.vector.bn_aggr(moments[:, q, :], stats[:, q, :]).then_inc(moments_done, 1)
                elif slot == 2 and step < 4:
                    dve.wait_ge(moments_done, (n + 1) * QT)
                    nc.vector.scalar_tensor_tensor(
                        out=acc[:, step, :], in0=acc[:, step, :], scalar=moments[:, step, 0:1], in1=gamma_b[:, :],
                        op0=ALU.subtract, op1=ALU.mult).then_inc(centered, 1)
                elif slot == 2:
                    q = step - 4
                    dve.wait_ge(rstd_done, n + 1)
                    dve.wait_ge(centered, n * QT + q + 1)
                    nc.vector.scalar_tensor_tensor(
                        out=acc[:, q, :], in0=acc[:, q, :], scalar=rstd[:, q:q + 1], in1=beta_b[:, :],
                        op0=ALU.mult, op1=ALU.add).then_inc(normed, 1)

            def prologue(g):
                group[0] = g
                if g == 0:
                    dve.wait_ge(consts_in, 6 * DMA)
                n = g * B
                for i, w in enumerate("qkvo"):
                    dve.wait_ge(w_hi_done, 4 * g + i + 1)
                    nc.vector.tensor_tensor(w_lo[w][:, :, :], probs[:, i % 2, :, :], w_hi[w][:, :, :],
                                            ALU.subtract).then_inc(w_split, 1)
                for p in range(2):
                    evacuate(n, "K", p)
                    evacuate(n, "Q", p)
                for h in range(2):
                    for q in range(QT):
                        mask_and_max(n, h, q)
                    if h == 0:
                        invert_sums(n, 0, 0)
                        invert_sums(n, 0, 1)

            def body(g, b, first, last):
                it = b + g * B
                for slot in range(GH):
                    for step in range(8):
                        if step < 4:
                            transposed_lo(it, slot, step)
                        elif head_at(it, slot + 2, last)[0] is not None:
                            mask_and_max(*head_at(it, slot + 2, last), step - 4)
                        if step == 1 and slot > 0:
                            add_context(it, slot - 1)
                        n, h = head_at(it, slot + 1, last)
                        if n is not None and step in (1, 3):
                            invert_sums(n, h, (step - 1) // 2)
                        for kind, k in fills(slot, step, first, last):
                            evacuate(batch_of(it, kind, k), kind, k)
                        if g == 1 and not first and slot in (1, 2):
                            layer_norm(it - 1, slot, step)
                add_context(it, GH - 1)

            def epilogue(g):
                it = g * B + B - 1
                for q in range(QT):
                    evacuate(it, "B", q)
                if g == 1:
                    for slot in (1, 2):
                        for step in range(8):
                            layer_norm(it, slot, step)

            batches(dve, prologue, body, epilogue)

        @block.gpsimd
        def _(pool):
            nc.gpsimd.sem_inc(stage_split, FREE_STAGES)
            nc.gpsimd.memset(ident[:, :], 0.0).then_inc(consts_set, 1)
            nc.gpsimd.memset(eps4[:, :], LN_EPS).then_inc(consts_set, 1)
            nc.gpsimd.memset(half4[:, :], -0.5).then_inc(consts_set, 1)
            pool.wait_ge(consts_set, 3)
            nc.gpsimd.affine_select(out=ident[:, :], in_=ident[:, :], compare_op=ALU.not_equal, fill=1.0, base=0,
                                    pattern=[[-1, P]], channel_multiplier=1).then_inc(consts_set, 1)

            def split_staged(n, kind, k):
                i = staged_no(n, kind, k)
                wait_alone(pool, staged, i)
                if kind == "X":
                    hi, lo = (z[:, :, (k % KT) * P:(k % KT + 1) * P] for z in xT["c" if k < KT else "x"])
                    src = stage[:, k % 2, :].rearrange("p (t s) -> p t s", t=DT)
                else:
                    hi, lo = v_part(k, False), v_part(k, True)
                    src = stage[:, (NX + k) % 2, :].rearrange("p (j a e) -> p j a e", a=2, e=DH)
                nc.gpsimd.tensor_scalar(hi, src, 1.0, 1.0, ALU.mult, ALU.mult).then_inc(stage_hi, 1)
                pool.wait_ge(stage_hi, i)
                nc.gpsimd.tensor_tensor(lo, src, hi, ALU.subtract).then_inc(stage_split, 1)

            def negate_max(n, h, half):
                wait_alone(pool, masked, (n * GH + h) * QT + 2 * half + 2 + SCORE_BANKS)
                cols = slice(2 * half, 2 * half + 2)
                nc.gpsimd.tensor_scalar(neg_max[:, h % 2, cols], row_max[:, h % 2, cols], -1.0, 1.0, ALU.mult,
                                        ALU.mult).then_inc(max_negated, 1)

            def normalize(n, h, half):
                wait_alone(pool, sum_inverted, (n * GH + h) * 2 + half + 1)
                for q in (2 * half, 2 * half + 1):
                    nc.gpsimd.tensor_scalar(probs[:, h % 2, q, :], probs[:, h % 2, q, :], inv_sum[:, h % 2, q:q + 1],
                                            1.0, ALU.mult, ALU.mult).then_inc(p_ready, 1)

            def split_context(it, p):
                i = it * PAIRS + p + 1
                wait_alone(pool, ctx_added, it * GH + 2 * p + 2 + CTX_BANKS)
                nc.gpsimd.tensor_scalar(ctxT_hi[:, p % 2, :], ctxT[:, :], 1.0, 1.0, ALU.mult,
                                        ALU.mult).then_inc(ctx_hi_done, 1)
                pool.wait_ge(ctx_hi_done, i)
                nc.gpsimd.tensor_tensor(ctxT_lo[:, p % 2, :], ctxT[:, :], ctxT_hi[:, p % 2, :],
                                        ALU.subtract).then_inc(ctx_split, 1)

            def add_bo(it, q):
                pool.wait_ge(acc_in[q], (it + 1) * DMA)
                nc.gpsimd.tensor_tensor(acc[:, q, :], acc[:, q, :], bo_b[:, :], ALU.add).then_inc(bo_added, 1)

            def inverse_deviation(it):
                n = it - B
                pool.wait_ge(moments_done, (n + 1) * QT)
                nc.gpsimd.tensor_tensor(var_eps[:, :], moments[:, :, 1], eps4[:, :], ALU.add).then_inc(eps_added, 1)
                pool.wait_ge(eps_added, n + 1)
                nc.gpsimd.tensor_tensor(rstd[:, :], var_eps[:, :], half4[:, :], ALU.pow).then_inc(rstd_done, 1)

            def prologue(g):
                if g == 0:
                    pool.wait_ge(consts_in, 6 * DMA)
                n = g * B
                for j in range(NX):
                    split_staged(n, "X", j)
                for t in range(KT):
                    split_staged(n, "V", t)
                for half in range(2):
                    negate_max(n, 0, half)
                for half in range(2):
                    normalize(n, 0, half)
                negate_max(n, 1, 0)

            def body(g, b, first, last):
                it = b + g * B
                for slot in range(GH):
                    for step in range(8):
                        for at, ahead, work, half in ((0, 1, negate_max, 1), (2, 1, normalize, 0),
                                                      (4, 1, normalize, 1), (6, 2, negate_max, 0)):
                            n, h = head_at(it, slot + ahead, last)
                            if step == at and n is not None:
                                work(n, h, half)
                        if step == 2 and slot in (2, 4, 6):
                            split_context(it, slot // 2 - 1)
                        if g == 0 and slot == 3 and step < 4:
                            add_bo(it, step)
                        if g == 1 and not first and slot == 2 and step == 0:
                            inverse_deviation(it - 1)
                        for kind, k in fills(slot, step, first, last):
                            if kind in "XV":
                                split_staged(batch_of(it, kind, k), kind, k)
                split_context(it, PAIRS - 1)

            def epilogue(g):
                if g == 1:
                    inverse_deviation(g * B + B - 1)

            batches(pool, prologue, body, epilogue)


_INS = ['x', 'ctx_1024', 'mask_Bx1xSxS2_fk1', 'L0_xattn_Wq', 'L0_xattn_bq', 'L0_xattn_Wk', 'L0_xattn_bk',
        'L0_xattn_Wv', 'L0_xattn_bv', 'L0_xattn_Wo', 'L0_xattn_bo', 'L0_xattn_gamma', 'L0_xattn_beta']


def kernel(**inputs):
    import numpy as _np
    import concourse.bacc as _bacc
    from concourse import mybir as _mybir
    from concourse.bass_utils import run_bass_kernel_spmd as _run

    nc = _bacc.Bacc("TRN2", target_bir_lowering=False, num_devices=1, dynamic_dma_scratch_size=1024)
    arrays, args = {}, []
    for name in _INS:
        a = _np.ascontiguousarray(inputs[name])
        arrays[f"in_{name}"] = a
        args.append(nc.dram_tensor(f"in_{name}", a.shape, _mybir.dt.from_np(a.dtype), kind="ExternalInput").ap())
    args.append(nc.dram_tensor("out_0", (B, S, D), F32, kind="ExternalOutput").ap())
    cross_attention(nc, *args)
    r = _run(nc, [arrays], core_ids=[0])
    return r.results[0]["out_0"]
```

```python
from contextlib import ExitStack

import concourse.bass as bass
from concourse import mybir

F32 = mybir.dt.float32
F32R = mybir.dt.float32r
ALU = mybir.AluOpType
ACT = mybir.ActivationFunctionType

P = 128
B, S, D = 16, 512, 512
H, DH = 16, 64
GROUPS = 2
GH = H // GROUPS
GW = GH * DH
PAIRS = GH // 2
QT, KT, DT = S // P, S // P, D // P
SCORE_SCALE = 1.0 / 8.0
LN_EPS = 1e-05
RAW_SLOTS = 4
NX = QT + KT
NSTAGED = KT + KT
DMA = 16

SCORE_BANKS, PT_BANKS, FREE_STAGES = 2, 2, 2
CTX_BANKS = 1

FILL_PARTS = {"K": DT, "Q": DT, "V": DT, "O": PAIRS, "X": 1}
FILL_BANKS = 3
FILL_BANK = dict(zip(
    "O0 O1 O2 K2 Q2 O3 K3 Q3 X0 X1 X2 X3 X4 X5 X6 X7 K0 Q0 V0 K1 Q1 V1 V2 V3".split(),
    (2, 1, 0, 2, 1, 0, 2, 1, 0, 2, 1, 0, 2, 1, 0, 2, 1, 2, 0, 1, 2, 1, 2, 0)))


def whole(fill):
    return [(fill, part) for part in range(FILL_PARTS[fill[0]])]


SCHEDULE = [
    ([("O0", 0), ("O0", 1), ("O0", 2), ("O1", 0), ("O1", 1), ("O1", 2), ("O2", 0), ("O0", 3), ("O1", 3), ("O2", 1)],
     (1, 2, 2, 2, 1, 1, 1, 0)),
    ([("O2", 2), ("O2", 3)] + whole("K2") + whole("Q2"), (1, 2, 2, 2, 1, 1, 1, 0)),
    (whole("O3") + whole("K3"), (1, 2, 2, 2, 1, 0, 0, 0)),
    (whole("Q3") + whole("X0") + whole("X1") + whole("X2") + whole("X3"), (1, 2, 2, 1, 1, 1, 0, 0)),
    (whole("X4") + whole("X5") + whole("X6") + whole("X7") + whole("K0"), (1, 2, 2, 2, 1, 0, 0, 0)),
    (whole("Q0") + [("V0", 0), ("V0", 1), ("V0", 2)], (1, 2, 2, 2, 0, 0, 0, 0)),
    (whole("K1") + whole("Q1"), (1, 2, 2, 2, 1, 0, 0, 0)),
    ([("V1", 0), ("V1", 1), ("V1", 2), ("V2", 0), ("V2", 1), ("V2", 2), ("V0", 3), ("V1", 3), ("V3", 0), ("V3", 1),
      ("V2", 3), ("V3", 2), ("V3", 3)], (1, 2, 2, 1, 1, 3, 2, 1)),
]
PARTS = {}
for _slot, (_parts, _counts) in enumerate(SCHEDULE):
    for _step, _count in enumerate(_counts):
        PARTS[_slot, _step] = [(fill[0], int(fill[1]), part) for fill, part in _parts[:_count]]
        _parts = _parts[_count:]
    assert not _parts


def is_ahead(kind, k):
    return kind in "XV" or (kind in "KQ" and k < 2)


def parts_of(slot, step, first, last):
    return [p for p in PARTS[slot, step] if not (p[0] == "O" and first) and not (is_ahead(p[0], p[1]) and last)]


def fills(slot, step, first, last):
    return [(kind, k) for kind, k, part in parts_of(slot, step, first, last) if part == FILL_PARTS[kind] - 1]


def cross_attention(nc, x, c, mask, wq, bq, wk, bk, wv, bv, wo, bo, gamma, beta, out):
    ctx = ExitStack()
    with ctx:
        def sb(name, shape, dt=F32):
            return ctx.enter_context(nc.sbuf_tensor(name, shape, dt))

        def ps(name, shape):
            return ctx.enter_context(nc.psum_tensor(name, shape, F32))

        def sem(name):
            return ctx.enter_context(nc.semaphore(name))

        partial = nc.dram_tensor("partial", (B, S, D), F32, kind="Internal").ap()

        w_hi = {w: sb(f"w{w}_hi", [P, DT, GW], F32R) for w in "qkv"}
        w_lo = {w: sb(f"w{w}_lo", [P, DT, GW], F32R) for w in "qkv"}
        w_hi["o"] = sb("wo_hi", [P, PAIRS, D], F32R)
        w_lo["o"] = sb("wo_lo", [P, PAIRS, D], F32R)
        xT = {t: (sb(f"{t}T_hi", [P, DT, S], F32R), sb(f"{t}T_lo", [P, DT, S], F32R)) for t in "cx"}
        q_stack = sb("q_stack", [P, 2, 2, S], F32R)
        k_twice = sb("k_twice", [P, 2, 2, 2, S], F32R)
        v_sb = sb("v_sb", [P, KT, 2 * GW], F32R)
        mask_sb = sb("mask_sb", [P, QT, S])
        acc = sb("acc", [P, QT, D])
        raw = sb("raw", [P, RAW_SLOTS, D])
        stage = sb("stage", [P, FREE_STAGES, S])
        probs = sb("probs", [P, 2, QT, S])
        pT_hi = sb("pT_hi", [P, KT, S], F32R)
        pT_lo = sb("pT_lo", [P, KT, S], F32R)
        ctxT_hi = sb("ctxT_hi", [P, PAIRS, S], F32R)
        ctxT_lo = sb("ctxT_lo", [P, PAIRS, S], F32R)
        ctxT = sb("ctxT", [P, S])
        gamma_b, beta_b, bo_b = sb("gamma_b", [P, D]), sb("beta_b", [P, D]), sb("bo_b", [P, D])
        ident = sb("ident", [P, P])
        bias_col = {n: sb(f"b{n}_col", [P, GROUPS * PAIRS]) for n in "qkv"}
        row_max, neg_max = sb("row_max", [P, 2, QT]), sb("neg_max", [P, 2, QT])
        row_sum, inv_sum = sb("row_sum", [P, 2, QT]), sb("inv_sum", [P, 2, QT])
        stats, moments = sb("stats", [P, QT, 6]), sb("moments", [P, QT, 2])
        eps4, half4 = sb("eps4", [P, QT]), sb("half4", [P, QT])
        var_eps, rstd = sb("var_eps", [P, QT]), sb("rstd", [P, QT])

        score_ps = ps("score_ps", [P, SCORE_BANKS, S])
        pT_ps = ps("pT_ps", [P, PT_BANKS, S])
        ctx_ps = ps("ctx_ps", [P, S])
        fill_ps = ps("fill_ps", [P, FILL_BANKS, S])

        consts_in = sem("consts_in")
        consts_set = sem("consts_set")
        w_in = {w: sem(f"w_in_{w}") for w in "qkvo"}
        w_hi_done = sem("w_hi_done")
        w_split = sem("w_split")
        raw_in = [sem(f"raw_in{r}") for r in range(RAW_SLOTS)]
        mask_in = [sem(f"mask_in{q}") for q in range(QT)]
        acc_in = [sem(f"acc_in{q}") for q in range(QT)]
        stored = [sem(f"stored{q}") for q in range(QT)]
        x_ready = sem("x_ready")
        v_ready = sem("v_ready")
        staged = sem("staged")
        x_hi = sem("x_hi")
        x_lo = sem("x_lo")
        stage_hi = sem("stage_hi")
        stage_split = sem("stage_split")
        qk_ready = sem("qk_ready")
        qk_hi = sem("qk_hi")
        qk_lo = sem("qk_lo")
        k_dup = [[sem(f"k_dup{i}{a}") for a in "ab"] for i in range(2)]
        s_ready = sem("s_ready")
        masked = sem("masked")
        max_negated = sem("max_negated")
        exp_done = sem("exp_done")
        sum_inverted = sem("sum_inverted")
        p_ready = sem("p_ready")
        t_ready = sem("t_ready")
        pT_hi_done = sem("pT_hi_done")
        pT_split = sem("pT_split")
        pv_ready = sem("pv_ready")
        ctx_crossed = sem("ctx_crossed")
        ctx_added = sem("ctx_added")
        ctx_hi_done = sem("ctx_hi_done")
        ctx_split = sem("ctx_split")
        out_ready = sem("out_ready")
        acc_added = sem("acc_added")
        bo_added = sem("bo_added")
        stats_done = sem("stats_done")
        moments_done = sem("moments_done")
        eps_added = sem("eps_added")
        rstd_done = sem("rstd_done")
        centered = sem("centered")
        normed = sem("normed")
        waits_passed = sem("waits_passed")

        def staged_no(n, kind, k):
            return n * NSTAGED + (k if kind == "X" else KT + k) + 1

        def qk_no(n, kind, p):
            return n * 2 * PAIRS + 2 * p + (kind == "Q") + 1

        def out_no(n, q):
            return n * QT + q + 1

        def fill_read(n, kind, k):
            if kind == "X" and k >= KT:
                return x_lo, n * QT + k - KT + 1
            if kind in "XV":
                return staged, staged_no(n, kind, k)
            if kind in "KQ":
                return qk_lo, qk_no(n, kind, k)
            return acc_added, out_no(n, k)

        def batch_of(it, kind, k):
            if kind == "O":
                return it - 1
            return it + 1 if is_ahead(kind, k) else it

        def batches(eng, prologue, body, epilogue):
            for g in range(GROUPS):
                prologue(g)
                body(g, 0, True, False)
                with eng.Fori(1, B - 1) as b:
                    body(g, b, False, False)
                body(g, B - 1, False, True)
                epilogue(g)

        def wait_alone(eng, semaphore, value):
            eng.wait_ge(semaphore, value)
            if not isinstance(value, int):
                eng.sem_inc(waits_passed, 1)

        def head_at(it, h, last):
            if h < GH:
                return it, h
            return (None, None) if last else (it + 1, h - GH)

        def rows_of(t, half, tile):
            return xT[t][half][:, :, tile * P:(tile + 1) * P]

        def v_part(tile, lo):
            view = v_sb[:, tile, :].rearrange("p (j a e) -> p j a e", a=4, e=DH)
            return view[:, :, 1:3, :] if lo else view[:, :, 0:4:3, :]

        block = ctx.enter_context(nc.Block())

        @block.sync
        def _(sp):
            for n, vec in (("q", bq), ("k", bk), ("v", bv)):
                with nc.allow_non_contiguous_dma(reason="once, 1024 values to columns"):
                    sp.dma_start(bias_col[n][:, :], vec.rearrange("(j p) -> p j", p=P)).then_inc(consts_in, DMA)
            for dst, vec in ((gamma_b, gamma), (beta_b, beta), (bo_b, bo)):
                sp.dma_start(dst[:, :], vec.partition_broadcast(P)).then_inc(consts_in, DMA)

            def load_raw(n, b, j):
                if isinstance(n, int) and n * NX + j < RAW_SLOTS:
                    pass
                else:
                    sp.wait_ge(x_ready, n * NX + j - RAW_SLOTS + 1)
                src, t = (c, j) if j < KT else (x, j - KT)
                sp.dma_start(raw[:, j % RAW_SLOTS, :], src[b, t * P:(t + 1) * P, :]).then_inc(
                    raw_in[j % RAW_SLOTS], DMA)

            def duplicate_keys(n, p):
                sp.wait_ge(qk_lo, qk_no(n, "K", p))
                for ab, (a, z) in ((0, (slice(0, DH), slice(DH, P))), (1, (slice(DH, P), slice(0, DH)))):
                    sp.dma_start(k_twice[z, p % 2, ab, :, :].bitcast(F32),
                                  k_twice[a, p % 2, ab, :, :].bitcast(F32)).then_inc(k_dup[p % 2][ab], DMA)

            def load_mask(n, b, q):
                if not (isinstance(n, int) and n == 0):
                    sp.wait_ge(masked, (n * GH - 1) * QT + q + 1 + SCORE_BANKS)
                sp.dma_start(mask_sb[:, q, :], mask[b, 0, q * P:(q + 1) * P, :]).then_inc(mask_in[q], DMA)

            def load_acc(g, it, b, q):
                if not (isinstance(it, int) and it == 0):
                    sp.wait_ge(stored[q], it * DMA)
                src = (x, partial)[g]
                sp.dma_start(acc[:, q, :], src[b, q * P:(q + 1) * P, :]).then_inc(acc_in[q], DMA)

            def store(g, it, b, q):
                if g == 0:
                    sp.wait_ge(acc_added, out_no(it, q))
                else:
                    sp.wait_ge(normed, (it - B) * QT + q + 1)
                dst = (partial, out)[g]
                sp.dma_start(dst[b, q * P:(q + 1) * P, :], acc[:, q, :]).then_inc(stored[q], DMA)

            def prologue(g):
                if g:
                    sp.wait_ge(out_ready, out_no(g * B - 1, QT - 1))
                cols = slice(g * GW, (g + 1) * GW)
                for i, (w, mat) in enumerate((("q", wq), ("k", wk), ("v", wv), ("o", wo))):
                    if i >= 2:
                        sp.wait_ge(w_split, 4 * g + i - 1)
                    src = mat[cols, :].rearrange("(j p) n -> p j n", p=P) if w == "o" else \
                        mat[:, cols].rearrange("(j p) n -> p j n", p=P)
                    sp.dma_start(probs[:, i % 2, :, :], src).then_inc(w_in[w], DMA)
                    if i < 2:
                        for j in range(4 * i, 4 * i + 4):
                            if i == 0:
                                load_raw(g * B, 0, j)
                for j in range(RAW_SLOTS, NX):
                    load_raw(g * B, 0, j)
                for q in range(QT):
                    load_mask(g * B, 0, q)
                duplicate_keys(g * B, 0)
                duplicate_keys(g * B, 1)

            def body(g, b, first, last):
                it = b + g * B

                def renew_acc():
                    if not first:
                        for q in range(QT):
                            store(g, it - 1, b - 1, q)
                    for q in range(QT):
                        load_acc(g, it, b, q)

                if not last:
                    for j in range(RAW_SLOTS):
                        load_raw(it + 1, b + 1, j)
                duplicate_keys(it, 2)
                if g == 0:
                    renew_acc()
                duplicate_keys(it, 3)
                if not last:
                    for j in range(RAW_SLOTS, NX):
                        load_raw(it + 1, b + 1, j)
                    duplicate_keys(it + 1, 0)
                    for q in range(QT):
                        load_mask(it + 1, b + 1, q)
                    duplicate_keys(it + 1, 1)
                if g == 1:
                    renew_acc()

            def epilogue(g):
                for q in range(QT):
                    store(g, g * B + B - 1, B - 1, q)

            batches(sp, prologue, body, epilogue)
            for q in range(QT):
                sp.wait_ge(stored[q], GROUPS * B * DMA)

        @block.tensor
        def _(pe):
            def three_products(bank, lhs, rhs, tile, is_first, is_last):
                nc.tensor.matmul(bank, lhs(0, tile), rhs(0, tile), start=is_first, stop=False)
                nc.tensor.matmul(bank, lhs(1, tile), rhs(0, tile), start=False, stop=False)
                return nc.tensor.matmul(bank, lhs(0, tile), rhs(1, tile), start=False, stop=is_last)

            def fill(n, kind, k, part, free):
                is_first, is_last = part == 0, part == FILL_PARTS[kind] - 1
                if is_first and free is not None:
                    pe.wait_ge(*free)
                bank = fill_ps[:, FILL_BANK[f"{kind}{k}"], :]
                if kind == "X":
                    pe.wait_ge(raw_in[k % RAW_SLOTS], (n * (NX // RAW_SLOTS) + k // RAW_SLOTS + 1) * DMA)
                    for t in range(DT):
                        mm = nc.tensor.transpose(bank[:, t * P:(t + 1) * P], raw[:, k % RAW_SLOTS, t * P:(t + 1) * P],
                                                 ident[:, :])
                    mm.then_inc(x_ready, 1)
                elif kind in "KQ":
                    if (kind, k, part) == ("K", 0, 0):
                        pe.wait_ge(stage_split, staged_no(n, "X", KT - 1) + FREE_STAGES)
                    if (kind, k, part) == ("Q", 0, 0):
                        pe.wait_ge(x_lo, (n + 1) * QT)
                    w = kind.lower()
                    act = xT["x" if kind == "Q" else "c"]
                    mm = three_products(bank, lambda a, t: (w_hi, w_lo)[a][w][:, t, k * P:(k + 1) * P],
                                        lambda r, t: act[r][:, t, :], part, is_first, is_last)
                    if is_last:
                        mm.then_inc(qk_ready, 1)
                elif kind == "V":
                    mm = three_products(bank, lambda a, t: xT["c"][a][:, t, k * P:(k + 1) * P],
                                        lambda r, t: (w_hi, w_lo)[r]["v"][:, t, :], part, is_first, is_last)
                    if is_last:
                        mm.then_inc(v_ready, 1)
                else:
                    if k == 0:
                        pe.wait_ge(ctx_split, n * PAIRS + part + 1)
                    mm = three_products(bank, lambda a, t: (ctxT_hi, ctxT_lo)[a][:, t, k * P:(k + 1) * P],
                                        lambda r, t: (w_hi, w_lo)[r]["o"][:, t, :], part, is_first, is_last)
                    if is_last:
                        mm.then_inc(out_ready, 1)

            def scores(n, h, q):
                par, ab = (h // 2) % 2, h % 2
                if q == 0:
                    pe.wait_ge(qk_lo, qk_no(n, "Q", h // 2))
                    pe.wait_ge(k_dup[par][ab], (n * 2 + h // 4 + 1) * DMA)
                pe.wait_ge(masked, (n * GH + h) * QT + q + 1)
                bank = score_ps[:, q % SCORE_BANKS, :]
                qs = q_stack[:, par, ab, q * P:(q + 1) * P]
                nc.tensor.matmul(bank, qs, k_twice[:, par, ab, 0, :], start=True, stop=False)
                nc.tensor.matmul(bank, qs, k_twice[:, par, ab, 1, :], start=False, stop=True).then_inc(s_ready, 1)

            def transposes(it, h, t):
                if t == 0:
                    pe.wait_ge(p_ready, (it * GH + h + 1) * QT)
                pe.wait_ge(pT_split, (it * GH + h) * KT + t + 1)
                for q in range(QT):
                    mm = nc.tensor.transpose(pT_ps[:, t % PT_BANKS, q * P:(q + 1) * P],
                                             probs[:, h % 2, q, t * P:(t + 1) * P], ident[:, :])
                mm.then_inc(t_ready, 1)

            def values(it, h, t):
                if h == 0 and t == 0:
                    pe.wait_ge(stage_split, staged_no(it, "V", KT - 1) + FREE_STAGES)
                if t == 0:
                    pe.wait_ge(ctx_added, it * GH + h + 1)
                pe.wait_ge(pT_split, (it * GH + h) * KT + t + 1 + PT_BANKS)
                v = v_sb[:, t, h * P:(h + 1) * P]
                nc.tensor.matmul(ctx_ps[:, :], v, pT_hi[:, t, :], start=(t == 0), stop=False)
                mm = nc.tensor.matmul(ctx_ps[:, :], v, pT_lo[:, t, :], start=False, stop=(t == KT - 1))
                if t == KT - 1:
                    mm.then_inc(pv_ready, 1)

            users = {}

            def prologue(g):
                n = g * B
                if g == 0:
                    pe.wait_ge(consts_set, 4)
                users.clear()
                for kind, k in [("X", j) for j in range(NX)] + [("K", 0), ("Q", 0), ("K", 1), ("Q", 1)] + \
                        [("V", t) for t in range(KT)]:
                    bank = FILL_BANK[f"{kind}{k}"]
                    free = users.get(bank)
                    if free is None and g:
                        free = (acc_added, out_no(n - 1, QT - 1))
                    if (kind, k) == ("K", 0):
                        pe.wait_ge(w_split, 4 * g + 4)
                    for part in range(FILL_PARTS[kind]):
                        fill(n, kind, k, part, free)
                    users[bank] = fill_read(n, kind, k)
                for h in range(2):
                    for q in range(QT):
                        scores(n, h, q)

            def body(g, b, first, last):
                it = b + g * B
                users.clear()
                users.update((FILL_BANK[f"V{t}"], fill_read(it, "V", t)) for t in range(KT))
                for slot in range(GH):
                    for step in range(8):
                        if step < 4:
                            transposes(it, slot, step)
                        else:
                            values(it, slot, step - 4)
                            n, h = head_at(it, slot + 2, last)
                            if n is not None:
                                scores(n, h, step - 4)
                        for kind, k, part in parts_of(slot, step, first, last):
                            n = batch_of(it, kind, k)
                            bank = FILL_BANK[f"{kind}{k}"]
                            fill(n, kind, k, part, users[bank])
                            if part == FILL_PARTS[kind] - 1:
                                users[bank] = fill_read(n, kind, k)

            def epilogue(g):
                it = g * B + B - 1
                for q in range(QT):
                    bank = FILL_BANK[f"O{q}"]
                    for part in range(FILL_PARTS["O"]):
                        fill(it, "O", q, part, users[bank])
                    users[bank] = fill_read(it, "O", q)

            batches(pe, prologue, body, epilogue)

        @block.scalar
        def _(act):
            def evacuate(n, kind, k):
                bank = fill_ps[:, FILL_BANK[f"{kind}{k}"], :]
                if kind == "X" and k >= KT:
                    act.wait_ge(x_ready, n * NX + k + 1)
                    nc.scalar.activation(rows_of("x", 0, k - KT), bank.rearrange("p (t s) -> p t s", t=DT),
                                         ACT.Copy).then_inc(x_hi, 1)
                elif kind in "XV":
                    i = staged_no(n, kind, k)
                    act.wait_ge(*((x_ready, n * NX + k + 1) if kind == "X" else (v_ready, n * KT + k + 1)))
                    act.wait_ge(stage_split, i)
                    nc.scalar.activation(stage[:, k % FREE_STAGES, :], bank, ACT.Copy).then_inc(staged, 1)
                elif kind in "KQ":
                    act.wait_ge(qk_ready, qk_no(n, kind, k))
                    for ab, part in ((0, slice(0, DH)), (1, slice(DH, P))):
                        dst = k_twice[part, k % 2, ab, 0, :] if kind == "K" else q_stack[part, k % 2, ab, :]
                        last = nc.scalar.activation(dst, bank[part, :], ACT.Identity,
                                                    bias=bias_of(kind, n, k)[part, :])
                    last.then_inc(qk_hi, 1)

            group = [0]

            def bias_of(kind, n, k):
                col = group[0] * PAIRS + k
                return bias_col[kind.lower()][:, col:col + 1]

            def exponentials(n, h, half):
                act.wait_ge(max_negated, (n * GH + h) * 2 + half + 1)
                for q in (2 * half, 2 * half + 1):
                    nc.scalar.activation(probs[:, h % 2, q, :], probs[:, h % 2, q, :], ACT.Exp,
                                         bias=neg_max[:, h % 2, q:q + 1],
                                         accum_out=row_sum[:, h % 2, q:q + 1]).then_inc(exp_done, 1)

            def transposed_hi(it, h, t):
                act.wait_ge(t_ready, (it * GH + h) * KT + t + 1)
                nc.scalar.activation(pT_hi[:, t, :], pT_ps[:, t % PT_BANKS, :], ACT.Copy).then_inc(pT_hi_done, 1)

            def cross(it, h):
                act.wait_ge(pv_ready, it * GH + h + 1)
                if h % 2 == 0 and not (isinstance(it, int) and it == 0 and h == 0):
                    act.wait_ge(ctx_split, it * PAIRS + h // 2)
                dst, src = (slice(0, DH), slice(DH, P)) if h % 2 == 0 else (slice(DH, P), slice(0, DH))
                nc.scalar.activation(ctxT[dst, :], ctx_ps[src, :], ACT.Copy).then_inc(ctx_crossed, 1)

            def prologue(g):
                group[0] = g
                if g == 0:
                    act.wait_ge(consts_in, 6 * DMA)
                n = g * B
                for i, w in enumerate("qkvo"):
                    act.wait_ge(w_in[w], (g + 1) * DMA)
                    nc.scalar.activation(w_hi[w][:, :, :], probs[:, i % 2, :, :], ACT.Copy).then_inc(w_hi_done, 1)
                for j in range(NX):
                    evacuate(n, "X", j)
                for p in range(2):
                    evacuate(n, "K", p)
                    evacuate(n, "Q", p)
                for t in range(KT):
                    evacuate(n, "V", t)
                exponentials(n, 0, 0)
                exponentials(n, 0, 1)
                exponentials(n, 1, 0)

            def body(g, b, first, last):
                it = b + g * B
                for slot in range(GH):
                    for step in range(8):
                        if step < 4:
                            transposed_hi(it, slot, step)
                        if step == 0 and slot > 0:
                            cross(it, slot - 1)
                        for at, ahead, half in ((1, 1, 1), (7, 2, 0)):
                            n, h = head_at(it, slot + ahead, last)
                            if step == at and n is not None:
                                exponentials(n, h, half)
                        for kind, k in fills(slot, step, first, last):
                            evacuate(batch_of(it, kind, k), kind, k)
                cross(it, GH - 1)

            batches(act, prologue, body, lambda g: None)

        @block.vector
        def _(dve):
            nc.vector.sem_inc(masked, SCORE_BANKS)
            nc.vector.sem_inc(pT_split, PT_BANKS)
            nc.vector.sem_inc(ctx_added, CTX_BANKS)
            group = [0]

            def mask_and_max(n, h, q):
                if h == 0:
                    dve.wait_ge(mask_in[q], (n + 1) * DMA)
                wait_alone(dve, s_ready, (n * GH + h) * QT + q + 1)
                nc.vector.tensor_tensor_reduce(
                    out=probs[:, h % 2, q, :], in0=score_ps[:, q % SCORE_BANKS, :], in1=mask_sb[:, q, :],
                    scale=SCORE_SCALE, scalar=-3.0e38, op0=ALU.mult, op1=ALU.max,
                    accum_out=row_max[:, h % 2, q:q + 1]).then_inc(masked, 1)

            def invert_sums(n, h, half):
                dve.wait_ge(exp_done, (n * GH + h) * QT + 2 * half + 2)
                cols = slice(2 * half, 2 * half + 2)
                nc.vector.reciprocal(inv_sum[:, h % 2, cols], row_sum[:, h % 2, cols]).then_inc(sum_inverted, 1)

            def transposed_lo(it, h, t):
                dve.wait_ge(pT_hi_done, (it * GH + h) * KT + t + 1)
                nc.vector.tensor_tensor(pT_lo[:, t, :], pT_ps[:, t % PT_BANKS, :], pT_hi[:, t, :],
                                        ALU.subtract).then_inc(pT_split, 1)

            def add_context(it, h):
                dve.wait_ge(ctx_crossed, it * GH + h + 1)
                part = slice(0, DH) if h % 2 == 0 else slice(DH, P)
                col = group[0] * PAIRS + h // 2
                nc.vector.scalar_tensor_tensor(
                    out=ctxT[part, :], in0=ctx_ps[part, :], scalar=bias_col["v"][part, col:col + 1],
                    in1=ctxT[part, :], op0=ALU.add, op1=ALU.add).then_inc(ctx_added, 1)

            def evacuate(n, kind, k):
                bank = fill_ps[:, FILL_BANK[f"{kind}{k}"], :]
                if kind in "KQ":
                    dve.wait_ge(qk_hi, qk_no(n, kind, k))
                    col = group[0] * PAIRS + k
                    for ab, part, other in ((0, slice(0, DH), slice(DH, P)), (1, slice(DH, P), slice(0, DH))):
                        hi = k_twice[part, k % 2, ab, 0, :] if kind == "K" else q_stack[part, k % 2, ab, :]
                        lo = k_twice[part, k % 2, ab, 1, :] if kind == "K" else q_stack[other, k % 2, ab, :]
                        last = nc.vector.scalar_tensor_tensor(
                            out=lo, in0=bank[part, :], scalar=bias_col[kind.lower()][part, col:col + 1], in1=hi,
                            op0=ALU.add, op1=ALU.subtract)
                    last.then_inc(qk_lo, 1)
                elif kind == "X" and k >= KT:
                    dve.wait_ge(x_hi, n * QT + k - KT + 1)
                    nc.vector.tensor_tensor(rows_of("x", 1, k - KT), bank.rearrange("p (t s) -> p t s", t=DT),
                                            rows_of("x", 0, k - KT), ALU.subtract).then_inc(x_lo, 1)
                elif kind == "O":
                    dve.wait_ge(out_ready, out_no(n, k))
                    dve.wait_ge(acc_in[k], (n + 1) * DMA)
                    if group[0] == 0:
                        dve.wait_ge(bo_added, n * QT + k + 1)
                    nc.vector.tensor_tensor(acc[:, k, :], bank, acc[:, k, :], ALU.add).then_inc(acc_added, 1)

            def layer_norm(it, slot, step):
                n = it - B
                if slot == 3 and step < 4:
                    dve.wait_ge(acc_added, out_no(it, step))
                    nc.vector.bn_stats(stats[:, step, :], acc[:, step, :]).then_inc(stats_done, 1)
                elif slot == 3:
                    q = step - 4
                    wait_alone(dve, stats_done, n * QT + q + 1)
                    nc.vector.bn_aggr(moments[:, q, :], stats[:, q, :]).then_inc(moments_done, 1)
                elif slot == 5 and step >= 4:
                    q = step - 4
                    dve.wait_ge(moments_done, (n + 1) * QT)
                    nc.vector.scalar_tensor_tensor(
                        out=acc[:, q, :], in0=acc[:, q, :], scalar=moments[:, q, 0:1], in1=gamma_b[:, :],
                        op0=ALU.subtract, op1=ALU.mult).then_inc(centered, 1)
                elif slot == 7 and step < 4:
                    dve.wait_ge(rstd_done, n + 1)
                    dve.wait_ge(centered, n * QT + step + 1)
                    nc.vector.scalar_tensor_tensor(
                        out=acc[:, step, :], in0=acc[:, step, :], scalar=rstd[:, step:step + 1], in1=beta_b[:, :],
                        op0=ALU.mult, op1=ALU.add).then_inc(normed, 1)

            def prologue(g):
                group[0] = g
                if g == 0:
                    dve.wait_ge(consts_in, 6 * DMA)
                n = g * B
                for i, w in enumerate("qkvo"):
                    dve.wait_ge(w_hi_done, 4 * g + i + 1)
                    nc.vector.tensor_tensor(w_lo[w][:, :, :], probs[:, i % 2, :, :], w_hi[w][:, :, :],
                                            ALU.subtract).then_inc(w_split, 1)
                for j in range(KT, NX):
                    evacuate(n, "X", j)
                for p in range(2):
                    evacuate(n, "K", p)
                    evacuate(n, "Q", p)
                for h in range(2):
                    for q in range(QT):
                        mask_and_max(n, h, q)
                    if h == 0:
                        invert_sums(n, 0, 0)
                        invert_sums(n, 0, 1)

            def body(g, b, first, last):
                it = b + g * B
                for slot in range(GH):
                    for step in range(8):
                        if step < 4:
                            transposed_lo(it, slot, step)
                        elif head_at(it, slot + 2, last)[0] is not None:
                            mask_and_max(*head_at(it, slot + 2, last), step - 4)
                        if step == 1 and slot > 0:
                            add_context(it, slot - 1)
                        n, h = head_at(it, slot + 1, last)
                        if n is not None and step in (1, 3):
                            invert_sums(n, h, (step - 1) // 2)
                        for kind, k in fills(slot, step, first, last):
                            evacuate(batch_of(it, kind, k), kind, k)
                        if g == 1 and not first:
                            layer_norm(it - 1, slot, step)
                add_context(it, GH - 1)

            def epilogue(g):
                it = g * B + B - 1
                for q in range(QT):
                    evacuate(it, "O", q)
                if g == 1:
                    for slot in (3, 5, 7):
                        for step in range(8):
                            layer_norm(it, slot, step)

            batches(dve, prologue, body, epilogue)

        @block.gpsimd
        def _(pool):
            nc.gpsimd.sem_inc(stage_split, FREE_STAGES)
            nc.gpsimd.memset(ident[:, :], 0.0).then_inc(consts_set, 1)
            nc.gpsimd.memset(eps4[:, :], LN_EPS).then_inc(consts_set, 1)
            nc.gpsimd.memset(half4[:, :], -0.5).then_inc(consts_set, 1)
            pool.wait_ge(consts_set, 3)
            nc.gpsimd.affine_select(out=ident[:, :], in_=ident[:, :], compare_op=ALU.not_equal, fill=1.0, base=0,
                                    pattern=[[-1, P]], channel_multiplier=1).then_inc(consts_set, 1)

            def split_staged(n, kind, k):
                i = staged_no(n, kind, k)
                wait_alone(pool, staged, i)
                if kind == "X":
                    hi, lo = rows_of("c", 0, k), rows_of("c", 1, k)
                    src = stage[:, k % FREE_STAGES, :].rearrange("p (t s) -> p t s", t=DT)
                else:
                    hi, lo = v_part(k, False), v_part(k, True)
                    src = stage[:, k % FREE_STAGES, :].rearrange("p (j a e) -> p j a e", a=2, e=DH)
                nc.gpsimd.tensor_scalar(hi, src, 1.0, 1.0, ALU.mult, ALU.mult).then_inc(stage_hi, 1)
                pool.wait_ge(stage_hi, i)
                nc.gpsimd.tensor_tensor(lo, src, hi, ALU.subtract).then_inc(stage_split, 1)

            def negate_max(n, h, half):
                wait_alone(pool, masked, (n * GH + h) * QT + 2 * half + 2 + SCORE_BANKS)
                cols = slice(2 * half, 2 * half + 2)
                nc.gpsimd.tensor_scalar(neg_max[:, h % 2, cols], row_max[:, h % 2, cols], -1.0, 1.0, ALU.mult,
                                        ALU.mult).then_inc(max_negated, 1)

            def normalize(n, h, half):
                wait_alone(pool, sum_inverted, (n * GH + h) * 2 + half + 1)
                for q in (2 * half, 2 * half + 1):
                    nc.gpsimd.tensor_scalar(probs[:, h % 2, q, :], probs[:, h % 2, q, :], inv_sum[:, h % 2, q:q + 1],
                                            1.0, ALU.mult, ALU.mult).then_inc(p_ready, 1)

            def split_context(it, p):
                i = it * PAIRS + p + 1
                if p == 0 and not (isinstance(it, int) and it == 0):
                    pool.wait_ge(out_ready, out_no(it - 1, QT - 1))
                wait_alone(pool, ctx_added, it * GH + 2 * p + 2 + CTX_BANKS)
                nc.gpsimd.tensor_scalar(ctxT_hi[:, p, :], ctxT[:, :], 1.0, 1.0, ALU.mult,
                                        ALU.mult).then_inc(ctx_hi_done, 1)
                pool.wait_ge(ctx_hi_done, i)
                nc.gpsimd.tensor_tensor(ctxT_lo[:, p, :], ctxT[:, :], ctxT_hi[:, p, :],
                                        ALU.subtract).then_inc(ctx_split, 1)

            def add_bo(it, q):
                pool.wait_ge(acc_in[q], (it + 1) * DMA)
                nc.gpsimd.tensor_tensor(acc[:, q, :], acc[:, q, :], bo_b[:, :], ALU.add).then_inc(bo_added, 1)

            def inverse_deviation(it):
                n = it - B
                pool.wait_ge(moments_done, (n + 1) * QT)
                nc.gpsimd.tensor_tensor(var_eps[:, :], moments[:, :, 1], eps4[:, :], ALU.add).then_inc(eps_added, 1)
                pool.wait_ge(eps_added, n + 1)
                nc.gpsimd.tensor_tensor(rstd[:, :], var_eps[:, :], half4[:, :], ALU.pow).then_inc(rstd_done, 1)

            def prologue(g):
                if g == 0:
                    pool.wait_ge(consts_in, 6 * DMA)
                n = g * B
                for j in range(KT):
                    split_staged(n, "X", j)
                for t in range(KT):
                    split_staged(n, "V", t)
                for half in range(2):
                    negate_max(n, 0, half)
                for half in range(2):
                    normalize(n, 0, half)
                negate_max(n, 1, 0)

            def body(g, b, first, last):
                it = b + g * B
                for slot in range(GH):
                    for step in range(8):
                        for at, ahead, work, half in ((0, 1, negate_max, 1), (2, 1, normalize, 0),
                                                      (4, 1, normalize, 1), (6, 2, negate_max, 0)):
                            n, h = head_at(it, slot + ahead, last)
                            if step == at and n is not None:
                                work(n, h, half)
                        if step == 4 and slot in (2, 4, 6):
                            split_context(it, slot // 2 - 1)
                        if g == 0 and slot in (5, 6) and step in (5, 7):
                            add_bo(it, (slot - 5) * 2 + (step - 5) // 2)
                        if g == 1 and not first and slot == 4 and step == 0:
                            inverse_deviation(it - 1)
                        for kind, k in fills(slot, step, first, last):
                            if kind == "V" or (kind == "X" and k < KT):
                                split_staged(batch_of(it, kind, k), kind, k)
                split_context(it, PAIRS - 1)

            def epilogue(g):
                if g == 1:
                    inverse_deviation(g * B + B - 1)

            batches(pool, prologue, body, epilogue)


_INS = ['x', 'ctx_1024', 'mask_Bx1xSxS2_fk1', 'L0_xattn_Wq', 'L0_xattn_bq', 'L0_xattn_Wk', 'L0_xattn_bk',
        'L0_xattn_Wv', 'L0_xattn_bv', 'L0_xattn_Wo', 'L0_xattn_bo', 'L0_xattn_gamma', 'L0_xattn_beta']


def kernel(**inputs):
    import numpy as _np
    import concourse.bacc as _bacc
    from concourse import mybir as _mybir
    from concourse.bass_utils import run_bass_kernel_spmd as _run

    nc = _bacc.Bacc("TRN2", target_bir_lowering=False, num_devices=1, dynamic_dma_scratch_size=1024)
    arrays, args = {}, []
    for name in _INS:
        a = _np.ascontiguousarray(inputs[name])
        arrays[f"in_{name}"] = a
        args.append(nc.dram_tensor(f"in_{name}", a.shape, _mybir.dt.from_np(a.dtype), kind="ExternalInput").ap())
    args.append(nc.dram_tensor("out_0", (B, S, D), F32, kind="ExternalOutput").ap())
    cross_attention(nc, *args)
    r = _run(nc, [arrays], core_ids=[0])
    return r.results[0]["out_0"]
```

```python
from contextlib import ExitStack

import concourse.bass as bass
from concourse import mybir

F32 = mybir.dt.float32
F32R = mybir.dt.float32r
ALU = mybir.AluOpType
ACT = mybir.ActivationFunctionType

P = 128
B, S, D = 16, 512, 512
H, DH = 16, 64
GROUPS = 2
GH = H // GROUPS
GW = GH * DH
PAIRS = GH // 2
QT, KT, DT = S // P, S // P, D // P
SCORE_SCALE = 1.0 / 8.0
LN_EPS = 1e-05
RAW_SLOTS = 4
ROW_TILES = QT + KT
SPLIT_TILES = ROW_TILES + KT
LAST = GROUPS * B - 1
DMA = 16

SCORE_BANKS, PT_BANKS, CTX_BANKS = 2, 2, 1

FILL_PARTS = {"Q": DT, "K": DT, "V": DT, "O": PAIRS, "X": 1, "C": 1}
FILL_BANKS = 3
FILL_BANK = dict(zip(
    "O0 O1 O2 Q2 K2 O3 Q3 X0 K3 X1 X2 X3 C0 C1 Q0 C2 C3 K0 V0 Q1 K1 V1 V2 V3".split(),
    (1, 2, 0, 2, 1, 0, 2, 1, 0, 2, 1, 2, 0, 1, 2, 0, 1, 2, 0, 1, 2, 1, 2, 0)))


def whole(*names):
    return [(name[0], int(name[1]), part) for name in names for part in range(FILL_PARTS[name[0]])]


def some(name, *parts):
    return [(name[0], int(name[1]), part) for part in parts]


SCHEDULE = [
    (some("O0", 0, 1, 2) + some("O1", 0, 1, 2) + some("O2", 0) + some("O0", 3) + some("O1", 3) + some("O2", 1),
     (1, 2, 2, 2, 1, 1, 1, 0)),
    (some("O2", 2, 3) + whole("Q2", "K2"), (2, 2, 2, 2, 1, 1, 0, 0)),
    (whole("O3", "Q3"), (1, 2, 2, 2, 1, 0, 0, 0)),
    (whole("X0", "K3", "X1", "X2", "X3", "C0"), (2, 2, 2, 1, 0, 1, 1, 0)),
    (whole("C1", "Q0", "C2", "C3"), (2, 2, 1, 1, 0, 1, 0, 0)),
    (whole("K0") + some("V0", 0, 1, 2), (1, 2, 1, 1, 1, 1, 0, 0)),
    (whole("Q1", "K1"), (1, 2, 2, 1, 1, 1, 0, 0)),
    (some("V1", 0, 1, 2) + some("V2", 0, 1, 2) + some("V0", 3) + some("V1", 3) + some("V3", 0, 1) + some("V2", 3) +
     some("V3", 2, 3), (1, 2, 2, 1, 1, 3, 2, 1)),
]
PARTS = {}
for _slot, (_parts, _counts) in enumerate(SCHEDULE):
    assert sum(_counts) == len(_parts)
    for _step, _count in enumerate(_counts):
        PARTS[_slot, _step], _parts = _parts[:_count], _parts[_count:]

END_PARTS = {(slot, 1 + q): ("O", q, part) for part, slot in enumerate((4, 5, 7)) for q in range(FILL_BANKS)}

LN_STEPS = {
    (1, 4): ("stats", 0), (1, 6): ("stats", 1), (2, 0): ("aggregate", 0), (2, 1): ("stats", 2), (2, 2): ("aggregate", 1),
    (2, 5): ("aggregate", 2), (2, 6): ("stats", 3), (3, 0): ("aggregate", 3),
    (5, 5): ("center", 0), (5, 6): ("center", 1), (5, 7): ("center", 2), (7, 0): ("center", 3),
    (7, 1): ("scale", 0), (7, 2): ("scale", 1), (7, 5): ("scale", 2), (7, 6): ("scale", 3)}


def fills_for(slot, step, start, end, turn):
    return sorted((f for at in range(8) for f in fills(slot, at, start, end) if turn(f[0], at) == step),
                  key=lambda f: f[0] in "QK")


def scalar_turn(kind, at):
    return at + 1 if kind in "QK" and at < 3 else at


def vector_turn(kind, at):
    if kind in "QK":
        return min(max(4, at + 1), 7)
    return at + 1 if at == 0 or (kind == "O" and 4 <= at < 7) else at


POOL_SPLITS = {("K", 3): (3, 6), ("Q", 0): (5, 0)}

ADD_BO_AT = [(4, 0), (6, 0), (7, 0), (7, 2)]

PROLOGUE_FILLS = [("X", t) for t in range(QT)] + [("C", t) for t in range(KT)] + \
    [("Q", 0), ("K", 0), ("Q", 1), ("K", 1)] + [("V", t) for t in range(KT)]
PROLOGUE_WEIGHTS = {("C", 0): "q", ("Q", 0): "k", ("K", 0): "v"}


def is_ahead(kind, k):
    return kind in "XCV" or (kind in "KQ" and k < 2)


def parts_of(slot, step, start, end):
    return [p for p in PARTS[slot, step] if not (p[0] == "O" and start) and not (is_ahead(p[0], p[1]) and end)]


def fills(slot, step, start, end):
    return [(kind, k) for kind, k, part in parts_of(slot, step, start, end) if part == FILL_PARTS[kind] - 1]


WEIGHT_ORDER = ("qkvo", "vqko")
WEIGHTS_AT = {(0, 6): ("v", 0), (1, 4): ("v", 1), (2, 6): ("q", 0), (3, 3): ("q", 1), (3, 7): ("k", 0), (4, 4): ("k", 1)}
OUT_WEIGHTS_AT = {(4, 4): ("o", 0), (5, 4): ("o", 1)}


def weights_at(g, slot, step, first, last):
    table = WEIGHTS_AT if last and g < GROUPS - 1 else OUT_WEIGHTS_AT if first else {}
    return [table[slot, step]] if (slot, step) in table else []


def weight_no(g, w, half):
    return 8 * g + 2 * WEIGHT_ORDER[g].index(w) + half + 1


def cross_attention(nc, x, c, mask, wq, bq, wk, bk, wv, bv, wo, bo, gamma, beta, out):
    ctx = ExitStack()
    with ctx:
        def sb(name, shape, dt=F32):
            return ctx.enter_context(nc.sbuf_tensor(name, shape, dt))

        def ps(name, shape):
            return ctx.enter_context(nc.psum_tensor(name, shape, F32))

        def sem(name):
            return ctx.enter_context(nc.semaphore(name))

        partial = nc.dram_tensor("partial", (B, S, D), F32, kind="Internal").ap()

        w_hi = {w: sb(f"w{w}_hi", [P, DT, GW], F32R) for w in "qkv"}
        w_lo = {w: sb(f"w{w}_lo", [P, DT, GW], F32R) for w in "qkv"}
        w_hi["o"] = sb("wo_hi", [P, PAIRS, D], F32R)
        w_lo["o"] = sb("wo_lo", [P, PAIRS, D], F32R)
        xT = {t: (sb(f"{t}T_hi", [P, DT, S], F32R), sb(f"{t}T_lo", [P, DT, S], F32R)) for t in "cx"}
        q_stack = sb("q_stack", [P, 2, 2, S], F32R)
        k_twice = sb("k_twice", [P, 2, 2, 2, S], F32R)
        v_sb = sb("v_sb", [P, KT, 2 * GW], F32R)
        mask_sb = sb("mask_sb", [P, QT, S])
        acc = sb("acc", [P, QT, D])
        raw = sb("raw", [P, RAW_SLOTS, D])
        probs = sb("probs", [P, 2, QT, S])
        pT_hi = sb("pT_hi", [P, KT, S], F32R)
        pT_lo = sb("pT_lo", [P, KT, S], F32R)
        ctxT_hi = sb("ctxT_hi", [P, PAIRS, S], F32R)
        ctxT_lo = sb("ctxT_lo", [P, PAIRS, S], F32R)
        ctxT = sb("ctxT", [P, S])
        gamma_b, beta_b, bo_b = sb("gamma_b", [P, D]), sb("beta_b", [P, D]), sb("bo_b", [P, D])
        ident = sb("ident", [P, P])
        bias_col = {n: sb(f"b{n}_col", [P, GROUPS * PAIRS]) for n in "qkv"}
        row_max, neg_max = sb("row_max", [P, 2, QT]), sb("neg_max", [P, 2, QT])
        row_sum, inv_sum = sb("row_sum", [P, 2, QT]), sb("inv_sum", [P, 2, QT])
        w_stage = sb("w_stage", [P, DT // 2, GW])
        pair_stage = sb("pair_stage", [P, S])
        stats, moments = sb("stats", [P, QT, 6]), sb("moments", [P, QT, 2])
        eps4, half4 = sb("eps4", [P, QT]), sb("half4", [P, QT])
        var_eps, rstd = sb("var_eps", [P, QT]), sb("rstd", [P, QT])

        score_ps = ps("score_ps", [P, SCORE_BANKS, S])
        pT_ps = ps("pT_ps", [P, PT_BANKS, S])
        ctx_ps = ps("ctx_ps", [P, S])
        fill_ps = ps("fill_ps", [P, FILL_BANKS, S])

        bias_in = sem("bias_in")
        rows_in = sem("rows_in")
        consts_set = sem("consts_set")
        w_in = [sem(f"w_in{i}") for i in range(5)]
        w_rounded = sem("w_rounded")
        w_split = sem("w_split")
        raw_in = [sem(f"raw_in{r}") for r in range(RAW_SLOTS)]
        mask_in = [sem(f"mask_in{q}") for q in range(QT)]
        acc_in = [sem(f"acc_in{q}") for q in range(QT)]
        stored = [sem(f"stored{q}") for q in range(QT)]
        x_ready = sem("x_ready")
        v_ready = sem("v_ready")
        tile_hi = sem("tile_hi")
        tile_lo = sem("tile_lo")
        qk_ready = {w: sem(f"{w}_ready") for w in "QK"}
        qk_hi = {w: sem(f"{w}_hi") for w in "QK"}
        qk_lo = {w: sem(f"{w}_lo") for w in "QK"}
        qk_lo_pool = {w: sem(f"{w}_lo_pool") for w in "QK"}
        k_dup = [[sem(f"k_dup{i}{a}") for a in "ab"] for i in range(2)]
        s_ready = sem("s_ready")
        masked = sem("masked")
        max_negated = sem("max_negated")
        exp_done = sem("exp_done")
        sum_inverted = sem("sum_inverted")
        p_ready = sem("p_ready")
        t_ready = sem("t_ready")
        pT_hi_done = sem("pT_hi_done")
        pT_split = sem("pT_split")
        pv_ready = sem("pv_ready")
        ctx_crossed = sem("ctx_crossed")
        ctx_added = sem("ctx_added")
        ctx_hi_done = sem("ctx_hi_done")
        ctx_split = sem("ctx_split")
        out_ready = sem("out_ready")
        acc_added = sem("acc_added")
        bo_added = sem("bo_added")
        stats_done = sem("stats_done")
        moments_done = sem("moments_done")
        eps_added = sem("eps_added")
        rstd_done = sem("rstd_done")
        centered = sem("centered")
        normed = sem("normed")
        waits_passed = sem("waits_passed")

        def tile_no(n, kind, k):
            return n * SPLIT_TILES + "XCV".index(kind) * KT + k + 1

        def pair_no(n, p):
            return n * PAIRS + p + 1

        def pair_split(n, kind, p):
            if (kind, p) in POOL_SPLITS:
                return qk_lo_pool[kind], 2 * (n + 1)
            rank = [i for i in range(PAIRS) if (kind, i) not in POOL_SPLITS].index(p)
            return qk_lo[kind], n * (PAIRS - 1) + rank + 1

        def out_no(n, q):
            return n * QT + q + 1

        def fill_read(n, kind, k):
            if kind in "XCV":
                return tile_lo, tile_no(n, kind, k)
            if (kind, k) in POOL_SPLITS:
                return qk_hi[kind], pair_no(n, k)
            if kind in "KQ":
                return pair_split(n, kind, k)
            return acc_added, out_no(n, k)

        def batch_of(it, kind, k):
            if kind == "O":
                return it - 1
            return it + 1 if is_ahead(kind, k) else it

        def weight_place(g, w, half):
            no = weight_no(g, w, half)
            if g == 0 and w in "qkv":
                i = (no - 1) % 4
                return probs[:, i // 2, 2 * (i % 2):2 * (i % 2) + 2, :], w_in[i], ((no - 1) // 4 + 1) * DMA
            return w_stage[:, :, :], w_in[4], (no - weight_no(0, "v", 1)) * DMA

        def group_of(g, kind, k, first, last):
            if kind == "O":
                return g - first
            return g + (is_ahead(kind, k) and last)

        def batches(eng, body):
            for g in range(GROUPS):
                body(g, 0, True, False)
                with eng.Fori(1, B - 1) as b:
                    body(g, b, False, False)
                body(g, B - 1, False, True)

        def wait_alone(eng, semaphore, value):
            eng.wait_ge(semaphore, value)
            if not isinstance(value, int):
                eng.sem_inc(waits_passed, 1)

        def head_at(it, h):
            if h < GH:
                return it, h
            return (None, None) if isinstance(it, int) and it == LAST else (it + 1, h - GH)

        def columns_of(kind, half, tile):
            return xT[kind.lower()][half][:, :, tile * P:(tile + 1) * P]

        def v_part(tile, half):
            view = v_sb[:, tile, :].rearrange("p (j a e) -> p j a e", a=4, e=DH)
            return view[:, :, 1:3, :] if half else view[:, :, 0:4:3, :]

        block = ctx.enter_context(nc.Block())

        @block.sync
        def _(sp):
            def load_raw(n, b, j):
                if not (isinstance(n, int) and n * ROW_TILES + j < RAW_SLOTS):
                    sp.wait_ge(x_ready, n * ROW_TILES + j - RAW_SLOTS + 1)
                src, t = (x, j) if j < QT else (c, j - QT)
                sp.dma_start(raw[:, j % RAW_SLOTS, :], src[b, t * P:(t + 1) * P, :]).then_inc(
                    raw_in[j % RAW_SLOTS], DMA)

            def duplicate_keys(n, p):
                sp.wait_ge(*pair_split(n, "K", p))
                for ab, (a, z) in ((0, (slice(0, DH), slice(DH, P))), (1, (slice(DH, P), slice(0, DH)))):
                    sp.dma_start(k_twice[z, p % 2, ab, :, :].bitcast(F32),
                                  k_twice[a, p % 2, ab, :, :].bitcast(F32)).then_inc(k_dup[p % 2][ab], DMA)

            def load_mask(n, b, q):
                if not (isinstance(n, int) and n == 0):
                    sp.wait_ge(masked, (n * GH - 1) * QT + q + 1 + SCORE_BANKS)
                sp.dma_start(mask_sb[:, q, :], mask[b, 0, q * P:(q + 1) * P, :]).then_inc(mask_in[q], DMA)

            def load_acc(g, it, b, q):
                if not (isinstance(it, int) and it == 0):
                    sp.wait_ge(stored[q], it * DMA)
                src = (x, partial)[g]
                sp.dma_start(acc[:, q, :], src[b, q * P:(q + 1) * P, :]).then_inc(acc_in[q], DMA)

            def store(g, it, b, q):
                if g == 0:
                    sp.wait_ge(acc_added, out_no(it, q))
                else:
                    sp.wait_ge(normed, (it - B) * QT + q + 1)
                dst = (partial, out)[g]
                sp.dma_start(dst[b, q * P:(q + 1) * P, :], acc[:, q, :]).then_inc(stored[q], DMA)

            def load_weight(g, w, half):
                no = weight_no(g, w, half)
                if g == 0 and w == "v":
                    sp.wait_ge(w_split, no - 4)
                elif no > weight_no(0, "o", 0):
                    sp.wait_ge(w_split, no - 1)
                cols = slice(g * GW, (g + 1) * GW)
                src = wo[cols, :] if w == "o" else {"q": wq, "k": wk, "v": wv}[w][:, cols]
                src = src.rearrange("(j p) n -> p j n", p=P)[:, 2 * half:2 * half + 2, :]
                place, arrived, _ = weight_place(g, w, half)
                sp.dma_start(place, src).then_inc(arrived, DMA)

            def prologue():
                for j in range(QT):
                    load_raw(0, 0, j)
                load_weight(0, "q", 0)
                load_weight(0, "q", 1)
                load_weight(0, "k", 0)
                load_weight(0, "k", 1)
                for j in range(QT, ROW_TILES):
                    load_raw(0, 0, j)
                load_weight(0, "v", 0)
                load_weight(0, "v", 1)
                for q in range(QT):
                    load_mask(0, 0, q)
                duplicate_keys(0, 0)
                duplicate_keys(0, 1)
                for dst, vec in ((bo_b, bo), (gamma_b, gamma), (beta_b, beta)):
                    sp.dma_start(dst[:, :], vec.partition_broadcast(P)).then_inc(rows_in, DMA)

            def body(g, b, first, last):
                it = b + g * B
                start, end = g == 0 and first, g == GROUPS - 1 and last
                next_b = 0 if last else b + 1
                new_weights = last and not end

                def renew_acc():
                    if not start:
                        for q in range(QT):
                            store(g - first, it - 1, B - 1 if first else b - 1, q)
                    for q in range(QT):
                        load_acc(g, it, b, q)

                if not end:
                    for j in range(RAW_SLOTS):
                        load_raw(it + 1, next_b, j)
                if new_weights:
                    load_weight(g + 1, "v", 0)
                    load_weight(g + 1, "v", 1)
                duplicate_keys(it, 2)
                if new_weights:
                    load_weight(g + 1, "q", 0)
                if g == 0:
                    renew_acc()
                if new_weights:
                    load_weight(g + 1, "q", 1)
                if not end:
                    for j in range(RAW_SLOTS, RAW_SLOTS + 2):
                        load_raw(it + 1, next_b, j)
                if new_weights:
                    load_weight(g + 1, "k", 0)
                if not end:
                    for j in range(RAW_SLOTS + 2, ROW_TILES):
                        load_raw(it + 1, next_b, j)
                if new_weights:
                    load_weight(g + 1, "k", 1)
                duplicate_keys(it, 3)
                if first:
                    for half in range(2):
                        load_weight(g, "o", half)
                if not end:
                    duplicate_keys(it + 1, 0)
                    for q in range(QT):
                        load_mask(it + 1, next_b, q)
                    duplicate_keys(it + 1, 1)
                if g == 1:
                    renew_acc()

            prologue()
            batches(sp, body)
            for q in range(QT):
                store(GROUPS - 1, LAST, B - 1, q)
            for q in range(QT):
                sp.wait_ge(stored[q], GROUPS * B * DMA)

        @block.tensor
        def _(pe):
            def three_products(bank, lhs, rhs, tile, is_first, is_last):
                nc.tensor.matmul(bank, lhs(0, tile), rhs(0, tile), start=is_first, stop=False)
                nc.tensor.matmul(bank, lhs(1, tile), rhs(0, tile), start=False, stop=False)
                return nc.tensor.matmul(bank, lhs(0, tile), rhs(1, tile), start=False, stop=is_last)

            def fill(n, kind, k, part, free):
                is_first, is_last = part == 0, part == FILL_PARTS[kind] - 1
                if is_first and free is not None:
                    pe.wait_ge(*free)
                if kind in "QKVO" and k == 0 and is_first and isinstance(n, int):
                    pe.wait_ge(w_split, weight_no(n // B, kind.lower(), 1))
                bank = fill_ps[:, FILL_BANK[f"{kind}{k}"], :]
                if kind in "XC":
                    j = k if kind == "X" else QT + k
                    pe.wait_ge(raw_in[j % RAW_SLOTS], (n * (ROW_TILES // RAW_SLOTS) + j // RAW_SLOTS + 1) * DMA)
                    for t in range(DT):
                        mm = nc.tensor.transpose(bank[:, t * P:(t + 1) * P], raw[:, j % RAW_SLOTS, t * P:(t + 1) * P],
                                                 ident[:, :])
                    mm.then_inc(x_ready, 1)
                elif kind in "KQ":
                    if k == 0 and is_first:
                        pe.wait_ge(tile_lo, tile_no(n, "X" if kind == "Q" else "C", KT - 1))
                    w = kind.lower()
                    act = xT["x" if kind == "Q" else "c"]
                    mm = three_products(bank, lambda a, t: (w_hi, w_lo)[a][w][:, t, k * P:(k + 1) * P],
                                        lambda r, t: act[r][:, t, :], part, is_first, is_last)
                    if is_last:
                        mm.then_inc(qk_ready[kind], 1)
                elif kind == "V":
                    mm = three_products(bank, lambda a, t: xT["c"][a][:, t, k * P:(k + 1) * P],
                                        lambda r, t: (w_hi, w_lo)[r]["v"][:, t, :], part, is_first, is_last)
                    if is_last:
                        mm.then_inc(v_ready, 1)
                else:
                    if k == 0:
                        pe.wait_ge(ctx_split, n * PAIRS + part + 1)
                    mm = three_products(bank, lambda a, t: (ctxT_hi, ctxT_lo)[a][:, t, k * P:(k + 1) * P],
                                        lambda r, t: (w_hi, w_lo)[r]["o"][:, t, :], part, is_first, is_last)
                    if is_last:
                        mm.then_inc(out_ready, 1)

            def scores(n, h, q):
                par, ab = (h // 2) % 2, h % 2
                if q == 0:
                    pe.wait_ge(*pair_split(n, "Q", h // 2))
                    pe.wait_ge(k_dup[par][ab], (n * 2 + h // 4 + 1) * DMA)
                pe.wait_ge(masked, (n * GH + h) * QT + q + 1)
                bank = score_ps[:, q % SCORE_BANKS, :]
                qs = q_stack[:, par, ab, q * P:(q + 1) * P]
                nc.tensor.matmul(bank, qs, k_twice[:, par, ab, 0, :], start=True, stop=False)
                nc.tensor.matmul(bank, qs, k_twice[:, par, ab, 1, :], start=False, stop=True).then_inc(s_ready, 1)

            def transposes(it, h, t):
                if t == 0:
                    pe.wait_ge(p_ready, (it * GH + h + 1) * QT)
                pe.wait_ge(pT_split, (it * GH + h) * KT + t + 1)
                for q in range(QT):
                    mm = nc.tensor.transpose(pT_ps[:, t % PT_BANKS, q * P:(q + 1) * P],
                                             probs[:, h % 2, q, t * P:(t + 1) * P], ident[:, :])
                mm.then_inc(t_ready, 1)

            def values(it, h, t):
                if h == 0 and t == 0:
                    pe.wait_ge(tile_lo, tile_no(it, "V", KT - 1))
                if t == 0:
                    pe.wait_ge(ctx_added, it * GH + h + 1)
                pe.wait_ge(pT_split, (it * GH + h) * KT + t + 1 + PT_BANKS)
                v = v_sb[:, t, h * P:(h + 1) * P]
                nc.tensor.matmul(ctx_ps[:, :], v, pT_hi[:, t, :], start=(t == 0), stop=False)
                mm = nc.tensor.matmul(ctx_ps[:, :], v, pT_lo[:, t, :], start=False, stop=(t == KT - 1))
                if t == KT - 1:
                    mm.then_inc(pv_ready, 1)

            users = {}

            def prologue():
                pe.wait_ge(consts_set, 4)
                for kind, k in PROLOGUE_FILLS:
                    bank = FILL_BANK[f"{kind}{k}"]
                    for part in range(FILL_PARTS[kind]):
                        fill(0, kind, k, part, users.get(bank))
                    users[bank] = fill_read(0, kind, k)
                    if (kind, k) in (("V", 1), ("V", 3)):
                        for q in range(QT):
                            scores(0, k // 2, q)

            def body(g, b, first, last):
                it = b + g * B
                start, end = g == 0 and first, g == GROUPS - 1 and last
                users.clear()
                users.update((FILL_BANK[f"V{t}"], fill_read(it, "V", t)) for t in range(KT))
                for slot in range(GH):
                    for step in range(8):
                        if step < 4:
                            transposes(it, slot, step)
                        else:
                            values(it, slot, step - 4)
                            n, h = head_at(it, slot + 2)
                            if n is not None:
                                scores(n, h, step - 4)
                        for kind, k, part in parts_of(slot, step, start, end):
                            n = batch_of(it, kind, k)
                            bank = FILL_BANK[f"{kind}{k}"]
                            fill(n, kind, k, part, users[bank])
                            if part == FILL_PARTS[kind] - 1:
                                users[bank] = fill_read(n, kind, k)
                        if end and (slot, step) in END_PARTS:
                            kind, k, part = END_PARTS[slot, step]
                            fill(it, kind, k, part, users[FILL_BANK[f"{kind}{k}"]])

            prologue()
            batches(pe, body)
            for q in range(QT):
                bank = FILL_BANK[f"O{q}"]
                for part in range(FILL_PARTS["O"]):
                    if ("O", q, part) not in END_PARTS.values():
                        fill(LAST, "O", q, part, users[bank])
                users[bank] = fill_read(LAST, "O", q)

        @block.scalar
        def _(act):
            def round_weight(g, w, half):
                place, arrived, value = weight_place(g, w, half)
                act.wait_ge(arrived, value)
                if g > 0 and w == "o" and half == 0:
                    act.wait_ge(out_ready, out_no(g * B - 1, QT - 1))
                nc.scalar.activation(w_hi[w][:, 2 * half:2 * half + 2, :], place, ACT.Copy).then_inc(w_rounded, 1)

            def evacuate(g, n, kind, k):
                bank = fill_ps[:, FILL_BANK[f"{kind}{k}"], :]
                if kind in "XC":
                    act.wait_ge(x_ready, n * ROW_TILES + (k if kind == "X" else QT + k) + 1)
                    nc.scalar.activation(columns_of(kind, 0, k), bank.rearrange("p (t s) -> p t s", t=DT),
                                         ACT.Copy).then_inc(tile_hi, 1)
                elif kind == "V":
                    act.wait_ge(v_ready, n * KT + k + 1)
                    nc.scalar.activation(v_part(k, 0), bank.rearrange("p (j a e) -> p j a e", a=2, e=DH),
                                         ACT.Copy).then_inc(tile_hi, 1)
                elif kind in "KQ":
                    act.wait_ge(qk_ready[kind], pair_no(n, k))
                    col = g * PAIRS + k
                    for ab, part in ((0, slice(0, DH)), (1, slice(DH, P))):
                        dst = k_twice[part, k % 2, ab, 0, :] if kind == "K" else q_stack[part, k % 2, ab, :]
                        last = nc.scalar.activation(dst, bank[part, :], ACT.Identity,
                                                    bias=bias_col[kind.lower()][part, col:col + 1])
                    if (kind, k) in POOL_SPLITS:
                        if kind == "K":
                            act.wait_ge(*pair_split(n, "Q", 0))
                        elif not (isinstance(n, int) and n == 0):
                            act.wait_ge(*pair_split(n - 1, "K", 3))
                        last = nc.scalar.activation(pair_stage[:, :], bank, ACT.Identity,
                                                    bias=bias_col[kind.lower()][:, col:col + 1])
                    last.then_inc(qk_hi[kind], 1)

            def exponentials(n, h, half):
                act.wait_ge(max_negated, (n * GH + h) * 2 + half + 1)
                for q in (2 * half, 2 * half + 1):
                    nc.scalar.activation(probs[:, h % 2, q, :], probs[:, h % 2, q, :], ACT.Exp,
                                         bias=neg_max[:, h % 2, q:q + 1],
                                         accum_out=row_sum[:, h % 2, q:q + 1]).then_inc(exp_done, 1)

            def transposed_hi(it, h, t):
                act.wait_ge(t_ready, (it * GH + h) * KT + t + 1)
                nc.scalar.activation(pT_hi[:, t, :], pT_ps[:, t % PT_BANKS, :], ACT.Copy).then_inc(pT_hi_done, 1)

            def cross(it, h):
                act.wait_ge(pv_ready, it * GH + h + 1)
                if h % 2 == 0 and not (isinstance(it, int) and it == 0 and h == 0):
                    act.wait_ge(ctx_split, it * PAIRS + h // 2)
                dst, src = (slice(0, DH), slice(DH, P)) if h % 2 == 0 else (slice(DH, P), slice(0, DH))
                nc.scalar.activation(ctxT[dst, :], ctx_ps[src, :], ACT.Copy).then_inc(ctx_crossed, 1)

            def prologue():
                for n, vec in (("q", bq), ("k", bk), ("v", bv)):
                    with nc.allow_non_contiguous_dma(reason="once, 1024 values to columns"):
                        act.dma_start(bias_col[n][:, :], vec.rearrange("(j p) -> p j", p=P)).then_inc(bias_in, DMA)
                for kind, k in PROLOGUE_FILLS:
                    if (kind, k) in PROLOGUE_WEIGHTS:
                        for half in range(2):
                            round_weight(0, PROLOGUE_WEIGHTS[kind, k], half)
                    if (kind, k) == ("Q", 0):
                        act.wait_ge(bias_in, 3 * DMA)
                    evacuate(0, 0, kind, k)
                exponentials(0, 0, 0)
                exponentials(0, 0, 1)
                exponentials(0, 1, 0)

            def body(g, b, first, last):
                it = b + g * B
                start, end = g == 0 and first, g == GROUPS - 1 and last
                for slot in range(GH):
                    for step in range(8):
                        if step < 4:
                            transposed_hi(it, slot, step)
                        if step == 0 and slot > 0:
                            cross(it, slot - 1)
                        for at, ahead, half in ((1, 1, 1), (7, 2, 0)):
                            n, h = head_at(it, slot + ahead)
                            if step == at and n is not None:
                                exponentials(n, h, half)
                        for kind, k in fills_for(slot, step, start, end, scalar_turn):
                            evacuate(group_of(g, kind, k, first, last), batch_of(it, kind, k), kind, k)
                        for w, half in weights_at(g, slot, step, first, last):
                            round_weight(g + last, w, half)
                cross(it, GH - 1)

            prologue()
            batches(act, body)

        @block.vector
        def _(dve):
            nc.vector.sem_inc(masked, SCORE_BANKS)
            nc.vector.sem_inc(pT_split, PT_BANKS)
            nc.vector.sem_inc(ctx_added, CTX_BANKS)

            def split_weight(g, w, half):
                dve.wait_ge(w_rounded, weight_no(g, w, half))
                part = slice(2 * half, 2 * half + 2)
                nc.vector.tensor_tensor(w_lo[w][:, part, :], weight_place(g, w, half)[0], w_hi[w][:, part, :],
                                        ALU.subtract).then_inc(w_split, 1)

            def mask_and_max(n, h, q):
                if h == 0:
                    dve.wait_ge(mask_in[q], (n + 1) * DMA)
                wait_alone(dve, s_ready, (n * GH + h) * QT + q + 1)
                nc.vector.tensor_tensor_reduce(
                    out=probs[:, h % 2, q, :], in0=score_ps[:, q % SCORE_BANKS, :], in1=mask_sb[:, q, :],
                    scale=SCORE_SCALE, scalar=-3.0e38, op0=ALU.mult, op1=ALU.max,
                    accum_out=row_max[:, h % 2, q:q + 1]).then_inc(masked, 1)

            def invert_sums(n, h, half):
                dve.wait_ge(exp_done, (n * GH + h) * QT + 2 * half + 2)
                cols = slice(2 * half, 2 * half + 2)
                nc.vector.reciprocal(inv_sum[:, h % 2, cols], row_sum[:, h % 2, cols]).then_inc(sum_inverted, 1)

            def transposed_lo(it, h, t):
                dve.wait_ge(pT_hi_done, (it * GH + h) * KT + t + 1)
                nc.vector.tensor_tensor(pT_lo[:, t, :], pT_ps[:, t % PT_BANKS, :], pT_hi[:, t, :],
                                        ALU.subtract).then_inc(pT_split, 1)

            def add_context(g, it, h):
                dve.wait_ge(ctx_crossed, it * GH + h + 1)
                part = slice(0, DH) if h % 2 == 0 else slice(DH, P)
                col = g * PAIRS + h // 2
                nc.vector.scalar_tensor_tensor(
                    out=ctxT[part, :], in0=ctx_ps[part, :], scalar=bias_col["v"][part, col:col + 1],
                    in1=ctxT[part, :], op0=ALU.add, op1=ALU.add).then_inc(ctx_added, 1)

            def evacuate(g, n, kind, k):
                bank = fill_ps[:, FILL_BANK[f"{kind}{k}"], :]
                if (kind, k) in POOL_SPLITS:
                    pass
                elif kind in "KQ":
                    dve.wait_ge(qk_hi[kind], pair_no(n, k))
                    col = g * PAIRS + k
                    for ab, part, other in ((0, slice(0, DH), slice(DH, P)), (1, slice(DH, P), slice(0, DH))):
                        hi = k_twice[part, k % 2, ab, 0, :] if kind == "K" else q_stack[part, k % 2, ab, :]
                        lo = k_twice[part, k % 2, ab, 1, :] if kind == "K" else q_stack[other, k % 2, ab, :]
                        last = nc.vector.scalar_tensor_tensor(
                            out=lo, in0=bank[part, :], scalar=bias_col[kind.lower()][part, col:col + 1], in1=hi,
                            op0=ALU.add, op1=ALU.subtract)
                    last.then_inc(qk_lo[kind], 1)
                elif kind in "XC":
                    dve.wait_ge(tile_hi, tile_no(n, kind, k))
                    nc.vector.tensor_tensor(columns_of(kind, 1, k), bank.rearrange("p (t s) -> p t s", t=DT),
                                            columns_of(kind, 0, k), ALU.subtract).then_inc(tile_lo, 1)
                elif kind == "V":
                    dve.wait_ge(tile_hi, tile_no(n, kind, k))
                    nc.vector.tensor_tensor(v_part(k, 1), bank.rearrange("p (j a e) -> p j a e", a=2, e=DH),
                                            v_part(k, 0), ALU.subtract).then_inc(tile_lo, 1)
                elif kind == "O":
                    dve.wait_ge(out_ready, out_no(n, k))
                    dve.wait_ge(acc_in[k], (n + 1) * DMA)
                    if g == 0:
                        dve.wait_ge(bo_added, n * QT + k + 1)
                    nc.vector.tensor_tensor(acc[:, k, :], bank, acc[:, k, :], ALU.add).then_inc(acc_added, 1)

            def layer_norm(it, operation, q):
                n = it - B
                if operation == "stats":
                    dve.wait_ge(acc_added, out_no(it, q))
                    nc.vector.bn_stats(stats[:, q, :], acc[:, q, :]).then_inc(stats_done, 1)
                elif operation == "aggregate":
                    wait_alone(dve, stats_done, n * QT + q + 1)
                    nc.vector.bn_aggr(moments[:, q, :], stats[:, q, :]).then_inc(moments_done, 1)
                elif operation == "center":
                    dve.wait_ge(moments_done, n * QT + q + 1)
                    nc.vector.scalar_tensor_tensor(
                        out=acc[:, q, :], in0=acc[:, q, :], scalar=moments[:, q, 0:1], in1=gamma_b[:, :],
                        op0=ALU.subtract, op1=ALU.mult).then_inc(centered, 1)
                else:
                    dve.wait_ge(rstd_done, n + 1)
                    dve.wait_ge(centered, n * QT + q + 1)
                    nc.vector.scalar_tensor_tensor(
                        out=acc[:, q, :], in0=acc[:, q, :], scalar=rstd[:, q:q + 1], in1=beta_b[:, :],
                        op0=ALU.mult, op1=ALU.add).then_inc(normed, 1)

            def prologue():
                for kind, k in PROLOGUE_FILLS:
                    if (kind, k) in PROLOGUE_WEIGHTS:
                        for half in range(2):
                            split_weight(0, PROLOGUE_WEIGHTS[kind, k], half)
                    if (kind, k) == ("Q", 0):
                        dve.wait_ge(bias_in, 3 * DMA)
                    evacuate(0, 0, kind, k)
                    if (kind, k) in (("V", 1), ("V", 3)):
                        for q in range(QT):
                            mask_and_max(0, k // 2, q)
                invert_sums(0, 0, 0)
                invert_sums(0, 0, 1)
                dve.wait_ge(rows_in, 3 * DMA)

            def body(g, b, first, last):
                it = b + g * B
                start, end = g == 0 and first, g == GROUPS - 1 and last
                for slot in range(GH):
                    for step in range(8):
                        if step < 4:
                            transposed_lo(it, slot, step)
                        elif head_at(it, slot + 2)[0] is not None:
                            mask_and_max(*head_at(it, slot + 2), step - 4)
                        if step == 1 and slot > 0:
                            add_context(g, it, slot - 1)
                        n, h = head_at(it, slot + 1)
                        if n is not None and step in (1, 2):
                            invert_sums(n, h, step - 1)
                        for kind, k in fills_for(slot, step, start, end, vector_turn):
                            evacuate(group_of(g, kind, k, first, last), batch_of(it, kind, k), kind, k)
                        for w, half in weights_at(g, slot, step, first, last):
                            split_weight(g + last, w, half)
                        if g == 1 and not first and (slot, step) in LN_STEPS:
                            layer_norm(it - 1, *LN_STEPS[slot, step])
                add_context(g, it, GH - 1)

            prologue()
            batches(dve, body)
            for q in range(QT):
                evacuate(GROUPS - 1, LAST, "O", q)
            for operation in ("stats", "aggregate", "center", "scale"):
                for q in range(QT):
                    layer_norm(LAST, operation, q)

        @block.gpsimd
        def _(pool):
            nc.gpsimd.memset(ident[:, :], 0.0).then_inc(consts_set, 1)
            nc.gpsimd.memset(eps4[:, :], LN_EPS).then_inc(consts_set, 1)
            nc.gpsimd.memset(half4[:, :], -0.5).then_inc(consts_set, 1)
            pool.wait_ge(consts_set, 3)
            nc.gpsimd.affine_select(out=ident[:, :], in_=ident[:, :], compare_op=ALU.not_equal, fill=1.0, base=0,
                                    pattern=[[-1, P]], channel_multiplier=1).then_inc(consts_set, 1)

            def split_pair(n, kind, k):
                if kind == "K":
                    pool.wait_ge(max_negated, (n * GH + POOL_SPLITS[kind, k][0] + 2) * 2 + 1)
                elif not (isinstance(n, int) and n == 0):
                    pool.wait_ge(max_negated, (n * GH + POOL_SPLITS[kind, k][0] + 1 - GH) * 2 + 2)
                pool.wait_ge(qk_hi[kind], pair_no(n, k))
                for ab, part, other in ((0, slice(0, DH), slice(DH, P)), (1, slice(DH, P), slice(0, DH))):
                    hi = k_twice[part, k % 2, ab, 0, :] if kind == "K" else q_stack[part, k % 2, ab, :]
                    lo = k_twice[part, k % 2, ab, 1, :] if kind == "K" else q_stack[other, k % 2, ab, :]
                    nc.gpsimd.tensor_tensor(lo, pair_stage[part, :], hi, ALU.subtract).then_inc(qk_lo_pool[kind], 1)
                    wait_alone(pool, qk_lo_pool[kind], 2 * n + ab + 1)

            def negate_max(n, h, half):
                wait_alone(pool, masked, (n * GH + h) * QT + 2 * half + 2 + SCORE_BANKS)
                cols = slice(2 * half, 2 * half + 2)
                nc.gpsimd.tensor_scalar(neg_max[:, h % 2, cols], row_max[:, h % 2, cols], -1.0, 1.0, ALU.mult,
                                        ALU.mult).then_inc(max_negated, 1)

            def normalize(n, h, half):
                wait_alone(pool, sum_inverted, (n * GH + h) * 2 + half + 1)
                for q in (2 * half, 2 * half + 1):
                    nc.gpsimd.tensor_scalar(probs[:, h % 2, q, :], probs[:, h % 2, q, :], inv_sum[:, h % 2, q:q + 1],
                                            1.0, ALU.mult, ALU.mult).then_inc(p_ready, 1)

            def split_context(it, p):
                i = it * PAIRS + p + 1
                if p == 0 and not (isinstance(it, int) and it == 0):
                    pool.wait_ge(out_ready, out_no(it - 1, QT - 1))
                wait_alone(pool, ctx_added, it * GH + 2 * p + 2 + CTX_BANKS)
                nc.gpsimd.tensor_scalar(ctxT_hi[:, p, :], ctxT[:, :], 1.0, 1.0, ALU.mult,
                                        ALU.mult).then_inc(ctx_hi_done, 1)
                pool.wait_ge(ctx_hi_done, i)
                nc.gpsimd.tensor_tensor(ctxT_lo[:, p, :], ctxT[:, :], ctxT_hi[:, p, :],
                                        ALU.subtract).then_inc(ctx_split, 1)

            def add_bo(it, q):
                pool.wait_ge(acc_in[q], (it + 1) * DMA)
                nc.gpsimd.tensor_tensor(acc[:, q, :], acc[:, q, :], bo_b[:, :], ALU.add).then_inc(bo_added, 1)

            def inverse_deviation(it):
                n = it - B
                pool.wait_ge(moments_done, (n + 1) * QT)
                nc.gpsimd.tensor_tensor(var_eps[:, :], moments[:, :, 1], eps4[:, :], ALU.add).then_inc(eps_added, 1)
                pool.wait_ge(eps_added, n + 1)
                nc.gpsimd.tensor_tensor(rstd[:, :], var_eps[:, :], half4[:, :], ALU.pow).then_inc(rstd_done, 1)

            def prologue():
                split_pair(0, "Q", 0)
                for half in range(2):
                    negate_max(0, 0, half)
                for half in range(2):
                    normalize(0, 0, half)
                negate_max(0, 1, 0)
                pool.wait_ge(rows_in, 3 * DMA)

            def body(g, b, first, last):
                it = b + g * B
                start, end = g == 0 and first, g == GROUPS - 1 and last
                for slot in range(GH):
                    for step in range(8):
                        for at, ahead, work, half in ((0, 1, negate_max, 1), (2, 1, normalize, 0),
                                                      (4, 1, normalize, 1), (6, 2, negate_max, 0)):
                            n, h = head_at(it, slot + ahead)
                            if step == at and n is not None:
                                work(n, h, half)
                        if slot == 0 and step == 0 and not start:
                            split_context(it - 1, PAIRS - 1)
                        if slot in (2, 4, 6) and step == 2:
                            split_context(it, slot // 2 - 1)
                        for (kind, k), at in POOL_SPLITS.items():
                            if (slot, step) == at and not (end and is_ahead(kind, k)):
                                split_pair(it + is_ahead(kind, k), kind, k)
                        if g == 0 and (slot, step) in ADD_BO_AT:
                            add_bo(it, ADD_BO_AT.index((slot, step)))
                        if g == 1 and not first and slot == 4 and step == 0:
                            inverse_deviation(it - 1)

            prologue()
            batches(pool, body)
            split_context(LAST, PAIRS - 1)
            inverse_deviation(LAST)


_INS = ['x', 'ctx_1024', 'mask_Bx1xSxS2_fk1', 'L0_xattn_Wq', 'L0_xattn_bq', 'L0_xattn_Wk', 'L0_xattn_bk',
        'L0_xattn_Wv', 'L0_xattn_bv', 'L0_xattn_Wo', 'L0_xattn_bo', 'L0_xattn_gamma', 'L0_xattn_beta']


def kernel(**inputs):
    import numpy as _np
    import concourse.bacc as _bacc
    from concourse import mybir as _mybir
    from concourse.bass_utils import run_bass_kernel_spmd as _run

    nc = _bacc.Bacc("TRN2", target_bir_lowering=False, num_devices=1, dynamic_dma_scratch_size=512)
    arrays, args = {}, []
    for name in _INS:
        a = _np.ascontiguousarray(inputs[name])
        arrays[f"in_{name}"] = a
        args.append(nc.dram_tensor(f"in_{name}", a.shape, _mybir.dt.from_np(a.dtype), kind="ExternalInput").ap())
    args.append(nc.dram_tensor("out_0", (B, S, D), F32, kind="ExternalOutput").ap())
    cross_attention(nc, *args)
    r = _run(nc, [arrays], core_ids=[0])
    return r.results[0]["out_0"]
```
